# Optimizing a Trainium2 kernel written in Bass

```python
import numpy as np
import jax
import jax.numpy as jnp

def _softmax(x, axis=-1):
    return jax.nn.softmax(x, axis=axis)

def _gelu(x):
    return jax.nn.gelu(x, approximate=True)

def _silu(x):
    return jax.nn.silu(x)

def _sigmoid(x):
    return jax.nn.sigmoid(x)

def _layernorm(x, axis=-1, eps=1e-05):
    m = jnp.mean(x, axis=axis, keepdims=True)
    v = jnp.var(x, axis=axis, keepdims=True)
    return (x - m) / jnp.sqrt(v + eps)

def _scatter_add(tgt, idx, src, axis=0):
    return tgt.at[idx].add(src)

def _segment_sum(src, seg, n):
    return jax.ops.segment_sum(src, seg, n)
kernel_name = 'mk_gnn_preln_d2_gnn_r32_af945f'

def setup_inputs(seed: int=0):
    np.random.seed(seed)
    _w = jnp.asarray

    def _rec_inputs():
        import jax
        import jax.numpy as jnp
        _gk = jax.random.key(seed)
        x = -0.0001006 + 1 * jax.random.normal(jax.random.fold_in(_gk, 1), (50000, 96), jnp.float32)
        src = jax.random.randint(jax.random.fold_in(_gk, 2), (25000,), 0, 50000, jnp.int32)
        dst = jnp.minimum((50000 * jax.random.uniform(jax.random.fold_in(_gk, 3), (25000,)) ** 2.0).astype(jnp.int32), 49999)
        _o = jnp.argsort(dst, stable=True)
        src = src[_o]
        dst = dst[_o]
        edge_attr_4 = 0.000714719 + 1.00021 * jax.random.normal(jax.random.fold_in(_gk, 11), (25000, 4), jnp.float32)
        edge_attr_96 = 5.93493e-05 + 1.00006 * jax.random.normal(jax.random.fold_in(_gk, 12), (25000, 96), jnp.float32)
        return (x, src, dst, edge_attr_4, edge_attr_96)
    x, src, dst, edge_attr_4, edge_attr_96 = _rec_inputs()

    def _L0_gnn_setup():
        import jax, jax.numpy as jnp
        import numpy as np
        N_NODES = 50000
        N_EDGES = 25000
        NIN = 96
        NOUT = 96
        key = jax.random.key(seed)
        ks = jax.random.split(key, 10)
        s = 1.0 / np.sqrt(NIN)
        so = 1.0 / np.sqrt(NOUT)
        return {'x': jax.random.normal(ks[0], (N_NODES, NIN), dtype=jnp.float32), 'edge_index': jax.random.randint(ks[1], (2, N_EDGES), 0, N_NODES, dtype=jnp.int64), 'edge_attr': jax.random.normal(ks[2], (N_EDGES, NIN), dtype=jnp.float32), 'W_edge': jax.random.uniform(ks[3], (NIN, NIN), jnp.float32, -s, s), 'b_edge': jax.random.uniform(ks[4], (NIN,), jnp.float32, -s, s), 'eps': jnp.zeros((), dtype=jnp.float32), 'W1': jax.random.uniform(ks[5], (NOUT, NIN), jnp.float32, -s, s), 'b1': jax.random.uniform(ks[6], (NOUT,), jnp.float32, -s, s), 'W2': jax.random.uniform(ks[7], (NOUT, NOUT), jnp.float32, -so, so), 'b2': jax.random.uniform(ks[8], (NOUT,), jnp.float32, -so, so)}
    _L0_gnn_all = _L0_gnn_setup()
    _L0_gnn_in = {k: v for k, v in _L0_gnn_all.items() if k in ('W_edge', 'b_edge', 'eps', 'W1', 'b1', 'W2', 'b2')}
    del _L0_gnn_all

    def _L1_gnn_setup():
        import jax, jax.numpy as jnp
        import numpy as np
        EPS = 1e-05

        def _mlp(h, W, b, gamma, beta):
            h = jax.nn.relu(h @ W + b)
            mu = jnp.mean(h, axis=0)
            var = jnp.mean(jnp.square(h - mu), axis=0)
            return gamma * (h - mu) * jax.lax.rsqrt(var + EPS) + beta
        key = jax.random.key(seed)
        ks = jax.random.split(key, 10)
        N, E, C_in, C_out, E_dim = (50000, 25000, 96, 96, 4)
        x = jax.random.normal(ks[0], (N, C_in), dtype=jnp.float32)
        edge_index = jax.random.randint(ks[1], (2, E), 0, N, dtype=jnp.int64)
        edge_attr = jax.random.normal(ks[2], (E, E_dim), dtype=jnp.float32)
        s = lambda fan_in: 1.0 / np.sqrt(fan_in)
        W_node = jax.random.uniform(ks[3], (C_in, C_out), jnp.float32, -s(C_in), s(C_in))
        b_node = jnp.zeros((C_out,), jnp.float32)
        g_node = jnp.ones((C_out,), jnp.float32)
        beta_node = jnp.zeros((C_out,), jnp.float32)
        W_edge = jax.random.uniform(ks[4], (E_dim, C_out), jnp.float32, -s(E_dim), s(E_dim))
        b_edge = jnp.zeros((C_out,), jnp.float32)
        g_edge = jnp.ones((C_out,), jnp.float32)
        beta_edge = jnp.zeros((C_out,), jnp.float32)
        M_in = 2 * C_in + C_out
        W_msg = jax.random.uniform(ks[5], (M_in, C_out), jnp.float32, -s(M_in), s(M_in))
        b_msg = jnp.zeros((C_out,), jnp.float32)
        g_msg = jnp.ones((C_out,), jnp.float32)
        beta_msg = jnp.zeros((C_out,), jnp.float32)
        return dict(x=x, edge_index=edge_index, edge_attr=edge_attr, W_node=W_node, b_node=b_node, g_node=g_node, beta_node=beta_node, W_edge=W_edge, b_edge=b_edge, g_edge=g_edge, beta_edge=beta_edge, W_msg=W_msg, b_msg=b_msg, g_msg=g_msg, beta_msg=beta_msg)
    _L1_gnn_all = _L1_gnn_setup()
    _L1_gnn_in = {k: v for k, v in _L1_gnn_all.items() if k in ('W_node', 'b_node', 'g_node', 'beta_node', 'W_edge', 'b_edge', 'g_edge', 'beta_edge', 'W_msg', 'b_msg', 'g_msg', 'beta_msg')}
    del _L1_gnn_all
    return {'x': x, 'src': src, 'dst': dst, 'edge_attr_4': edge_attr_4, 'edge_attr_96': edge_attr_96, 'L0_gnn_W_edge': _L0_gnn_in['W_edge'], 'L0_gnn_b_edge': _L0_gnn_in['b_edge'], 'L0_gnn_eps': _L0_gnn_in['eps'], 'L0_gnn_W1': _L0_gnn_in['W1'], 'L0_gnn_b1': _L0_gnn_in['b1'], 'L0_gnn_W2': _L0_gnn_in['W2'], 'L0_gnn_b2': _L0_gnn_in['b2'], 'L1_gnn_W_node': _L1_gnn_in['W_node'], 'L1_gnn_b_node': _L1_gnn_in['b_node'], 'L1_gnn_g_node': _L1_gnn_in['g_node'], 'L1_gnn_beta_node': _L1_gnn_in['beta_node'], 'L1_gnn_W_edge': _L1_gnn_in['W_edge'], 'L1_gnn_b_edge': _L1_gnn_in['b_edge'], 'L1_gnn_g_edge': _L1_gnn_in['g_edge'], 'L1_gnn_beta_edge': _L1_gnn_in['beta_edge'], 'L1_gnn_W_msg': _L1_gnn_in['W_msg'], 'L1_gnn_b_msg': _L1_gnn_in['b_msg'], 'L1_gnn_g_msg': _L1_gnn_in['g_msg'], 'L1_gnn_beta_msg': _L1_gnn_in['beta_msg']}

def reference(x, src, dst, edge_attr_4, edge_attr_96, L0_gnn_W_edge, L0_gnn_b_edge, L0_gnn_eps, L0_gnn_W1, L0_gnn_b1, L0_gnn_W2, L0_gnn_b2, L1_gnn_W_node, L1_gnn_b_node, L1_gnn_g_node, L1_gnn_beta_node, L1_gnn_W_edge, L1_gnn_b_edge, L1_gnn_g_edge, L1_gnn_beta_edge, L1_gnn_W_msg, L1_gnn_b_msg, L1_gnn_g_msg, L1_gnn_beta_msg):
    import jax
    import jax.numpy as jnp

    def _L0_gnn_ref(x, edge_index, edge_attr, W_edge, b_edge, eps, W1, b1, W2, b2):
        import jax, jax.numpy as jnp
        import numpy as np
        N_NODES = 50000
        N_EDGES = 25000
        NIN = 96
        NOUT = 96
        ea = edge_attr @ W_edge.T + b_edge
        src, dst = (edge_index[0], edge_index[1])
        msg = jax.nn.relu(x[src] + ea)
        aggr = jax.ops.segment_sum(msg, dst, num_segments=N_NODES)
        h = (1.0 + eps) * x + aggr
        h = jax.nn.relu(h @ W1.T + b1)
        return h @ W2.T + b2

    def _L1_gnn_ref(x, edge_index, edge_attr, W_node, b_node, g_node, beta_node, W_edge, b_edge, g_edge, beta_edge, W_msg, b_msg, g_msg, beta_msg):
        import jax, jax.numpy as jnp
        import numpy as np
        EPS = 1e-05

        def _mlp(h, W, b, gamma, beta):
            h = jax.nn.relu(h @ W + b)
            mu = jnp.mean(h, axis=0)
            var = jnp.mean(jnp.square(h - mu), axis=0)
            return gamma * (h - mu) * jax.lax.rsqrt(var + EPS) + beta
        node_feat = _mlp(x, W_node, b_node, g_node, beta_node)
        edge_feat = _mlp(edge_attr, W_edge, b_edge, g_edge, beta_edge)
        row, col = (edge_index[0], edge_index[1])
        message = jnp.concatenate([x[row], x[col], edge_feat], axis=1)
        message = _mlp(message, W_msg, b_msg, g_msg, beta_msg)
        agg = jax.ops.segment_sum(message, col, num_segments=node_feat.shape[0])
        return agg + node_feat
    edge_index = jnp.stack([src, dst])
    h = jnp.maximum(_layernorm(x, axis=-1), 0.0)
    x = x + _L0_gnn_ref(h, edge_index, edge_attr_96, L0_gnn_W_edge, L0_gnn_b_edge, L0_gnn_eps, L0_gnn_W1, L0_gnn_b1, L0_gnn_W2, L0_gnn_b2)
    h = jnp.maximum(_layernorm(x, axis=-1), 0.0)
    x = x + _L1_gnn_ref(h, edge_index, edge_attr_4, L1_gnn_W_node, L1_gnn_b_node, L1_gnn_g_node, L1_gnn_beta_node, L1_gnn_W_edge, L1_gnn_b_edge, L1_gnn_g_edge, L1_gnn_beta_edge, L1_gnn_W_msg, L1_gnn_b_msg, L1_gnn_g_msg, L1_gnn_beta_msg)
    return x

_drawn_inputs = setup_inputs


def setup_inputs(seed=0):
    import zlib

    import numpy as np

    out = dict(_drawn_inputs(seed))
    spreads = {'L1_gnn_b_node': (0.0, 0.1),
     'L1_gnn_g_node': (1.0, 0.2),
     'L1_gnn_beta_node': (0.0, 0.1),
     'L1_gnn_b_edge': (0.0, 0.1),
     'L1_gnn_g_edge': (1.0, 0.2),
     'L1_gnn_beta_edge': (0.0, 0.329),
     'L1_gnn_b_msg': (0.0, 0.1),
     'L1_gnn_g_msg': (1.0, 0.2),
     'L1_gnn_beta_msg': (0.0, 0.1)}
    factors = {'L0_gnn_b_edge': 2.79}
    for name, (base, spread) in spreads.items():
        noise = np.random.default_rng([zlib.crc32(name.encode()), seed]).standard_normal(out[name].shape)
        drawn = base * np.exp(spread * noise) if base else spread * noise
        out[name] = jnp.asarray(drawn.astype(out[name].dtype))
    for name, factor in factors.items():
        out[name] = (out[name] * factor).astype(out[name].dtype)
    return out
```

```python
from contextlib import ExitStack

import concourse.bass as bass
from concourse import mybir

FP32 = mybir.dt.float32
INT32 = mybir.dt.int32
ALU = mybir.AluOpType
ACT = mybir.ActivationFunctionType
AX = mybir.AxisListType

P = 128
NODES, EDGES, C, CE = 50000, 25000, 96, 4
LN_EPS = BN_EPS = 1e-5
G = 4
W = G * P
NT = -(-NODES // W) * G
NG = NT // G
ET = -(-EDGES // P)
EG = ET // G
TILES = NT + 1
DUMP = NT - 1
IDX = ET + 2 * G
EDGES_LAST = EDGES - (ET - 1) * P
EW_LAST = EDGES - (EG - 1) * W
NW_LAST = NODES - (NG - 1) * W
assert ET % G == 0 and G == 4 and DUMP * P >= NODES and EG % 2 == 1 and NG == 2 * EG
ZN = 72
assert TILES * C % ZN == 0
C1 = C + 1

START = 2


def done(g):
    return g + 1 + START


def two_back(g):
    return g + 1


def one_back(g):
    return g + 2


def landed(turn):
    return 16 * (turn + 1)


def pairs_landed(g, pair=0):
    return 16 * (g * 2 + pair)


def settle_waits(eng, mark):
    eng.sem_inc(mark, 1)


class Phase:

    def __init__(self, nc, name):
        self.nc, self.name, self.stack = nc, name, ExitStack()
        self.counts = []

    def __enter__(self):
        self.stack.__enter__()
        return self

    def __exit__(self, *a):
        return self.stack.__exit__(*a)

    def sb(self, name, shape, dt=FP32):
        return self.stack.enter_context(self.nc.sbuf_tensor(f"{self.name}_{name}", shape, dt))

    def ps(self, name, shape, dt=FP32):
        return self.stack.enter_context(self.nc.psum_tensor(f"{self.name}_ps_{name}", shape, dt))

    def sem(self, name):
        return self.stack.enter_context(self.nc.semaphore(f"{self.name}_{name}"))

    def sems(self, name, n=2):
        return [self.sem(f"{name}{i}") for i in range(n)]

    def count(self, name):
        s = self.sem(name)
        self.counts.append(s)
        return s

    def prime(self, eng):
        for s in self.counts:
            eng.sem_inc(s, START)


class Kept:
    pass


def tiles(g, n=G):
    return bass.ds(g * G, n) if not isinstance(g, int) else slice(g * G, g * G + n)


def span(start, n):
    return bass.ds(start, n) if not isinstance(start, int) else slice(start, start + n)


def edge_phase_0(nc, d, k):
    with Phase(nc, "e0") as ph:
        xs = ph.sb("xs", [P, 2, G, C])
        eaT = ph.sb("eaT", [C1, 2, W])
        ea4T = ph.sb("ea4T", [CE, 2, W])
        dr = ph.sb("dst_row", [P, 2, W], INT32)
        h = ph.sb("h", [P, 2, G, C])
        msg = ph.sb("msg", [P, 2, G, C])
        efT = ph.sb("efT", [C, 2, W])
        S = ph.sb("same_dst", [P, 2, G, 2 * P])
        tot = ph.sb("tot", [P, 2, G, C])
        junk = ph.sb("junk", [P, G, 2 * P], mybir.dt.bfloat16)
        first = ph.sb("first_mask", [P, 2, 2 * P])
        bn = ph.sb("bn", [P, 2, 3 * G, 6])
        mv = ph.sb("mean_var", [P, 2, 3 * G, 2])
        sd = ph.sb("std", [P, 2, 3 * G])
        rs = ph.sb("rstd", [P, 2, G])
        nb = ph.sb("nbias", [P, 2, G])
        earlier = ph.sb("earlier", [P, 2, G])
        dup = ph.sb("dup", [P, 2, G])
        srci = ph.sb("src_i", [P, IDX], INT32)
        dsti = ph.sb("dst_i", [P, IDX], INT32)
        lo = ph.sb("lo", [P, IDX], INT32)
        hi = ph.sb("hi", [P, IDX], INT32)
        dump = ph.sb("dump_less_row", [P, ET])
        dumpi = ph.sb("dump_i", [P, G], INT32)
        dumpf = ph.sb("dump_f", [P, G])
        gidx = ph.sb("gather_idx", [P, 2, G], INT32)
        sidx = ph.sb("scatter_idx", [P, 2, G], INT32)
        ZW = TILES * C // ZN
        zero = ph.sb("zero", [P, ZW])
        ps_pre = [ph.ps(f"pre{s}", [P, G, C]) for s in range(2)]
        ps_tot = [ph.ps(f"tot{s}", [P, G, C]) for s in range(2)]
        ps_ef = [ph.ps(f"ef{s}", [C, W]) for s in range(2)]

        const_in = ph.sem("const_in")
        idx_in = ph.sem("idx_in")
        zero_made, agg0_zeroed = ph.sem("zero_made"), ph.sem("agg0_zeroed")
        masks_made, masks_filled = ph.sem("masks_made"), ph.sem("masks_filled")
        rows_made = ph.sem("rows_made")
        ones_made = ph.sem("ones_made")
        ea_in, ea4_in, dr_in, x_in, xs_in = (ph.sems(n) for n in ("ea_in", "ea4_in", "dr_in", "x_in", "xs_in"))
        scattered = ph.sems("scattered")
        gidx_made = ph.sem("gidx_made")
        bn_made, mv_made = ph.count("bn_made"), ph.count("mv_made")
        std_made, rs_made, nb_made = ph.count("std_made"), ph.count("rs_made"), ph.count("nb_made")
        h_made, sum_made, msg_made = ph.count("h_made"), ph.count("sum_made"), ph.count("msg_made")
        S_made, earlier_made, dup_made = ph.count("S_made"), ph.count("earlier_made"), ph.count("dup_made")
        shift_made, sidx_made, sidx_copied = ph.count("shift_made"), ph.count("sidx_made"), ph.count("sidx_copied")
        pre_made, ef_made, tot_made = ph.count("pre_made"), ph.count("ef_made"), ph.count("tot_made")
        efr_made, efst_made, tot_out = ph.count("efr_made"), ph.count("efst_made"), ph.count("tot_out")

        xrows = d["x"].rearrange("p t c -> (p t) c")
        aggrows = d["agg0"].rearrange("p t c -> (p t) c")

        pool_mark, dve_mark = ph.sem("pool_mark"), ph.sem("dve_mark")

        with nc.Block() as block:

            @block.sync
            def _(sp):
                sp.dma_start(srci[:, 0:ET], d["src_col"]).then_inc(idx_in, 16)
                sp.dma_start(dsti[:, 0:ET], d["dst_col"]).then_inc(idx_in, 16)
                for to, of in ((k.w_e0[:, :], d["w_e0"]), (k.w_ef[:, :], d["w_ef"]), (k.b_ef[:, :], d["b_ef"]),
                               (k.one_eps[:, :], d["eps"].broadcast_to([P, 1])),
                               (k.w1[:, :], d["w1"]), (k.b1[:, :], d["b1"]), (k.w2[:, :], d["w2"]),
                               (k.w_node[:, :], d["w_node"]), (k.b_node[:, :], d["b_node"]),
                               (k.w_msg[:, :, :], d["w_msg"].rearrange("a i o -> i a o")),
                               (k.b_msg[C:C1, :], d["b_msg"]), (k.bn_gb[:, :], d["bn_gb"])):
                    sp.dma_start(to, of).then_inc(const_in, 16)
                def loads(g, s):
                    sp.wait_ge(pre_made, two_back(g))
                    sp.dma_start(eaT[0:C, s, :], d["eaT"][:, span(g * W, W)]).then_inc(ea_in[s], 16)
                    sp.wait_ge(ef_made, two_back(g))
                    sp.dma_start(ea4T[:, s, :], d["ea4T"][:, span(g * W, W)]).then_inc(ea4_in[s], 16)
                    sp.wait_ge(earlier_made, two_back(g))
                    sp.dma_start(dr[:, s, :], d["dst_row"][:, span(g * W, W)].broadcast_to([P, W])).then_inc(dr_in[s], 16)
                    sp.wait_ge(bn_made, two_back(g))
                    sp.dma_start(k.R[:, span(g * 2 * G, 2 * G), :], d["x"][:, span(g * 2 * G, 2 * G), :]).then_inc(x_in[s], 16)

                for g in range(2):
                    loads(g, g)
                sp.wait_ge(zero_made, 1)
                flat = d["agg0"].rearrange("p t c -> p (t c)")
                with sp.Fori(0, ZN) as i:
                    sp.dma_start(flat[:, bass.ds(i * ZW, ZW)], zero[:, :]).then_inc(agg0_zeroed, 16)
                with sp.Fori(1, EG // 2) as it:
                    for s in range(2):
                        loads(it * 2 + s, s)
                loads(EG - 1, 0)

            @block.gpsimd
            def _(pool):
                ph.prime(pool)
                pool.memset(zero[:, :], 0.0).then_inc(zero_made, 1)
                pool.memset(k.ident[:, :], 0.0).then_inc(masks_filled, 1)
                pool.memset(first[:, :, :], 1.0).then_inc(masks_filled, 1)
                pool.wait_ge(masks_filled, 2)
                pool.affine_select(out=k.ident[:, :], in_=k.ident[:, :], compare_op=ALU.not_equal, fill=1.0,
                                   base=0, pattern=[[-1, P]], channel_multiplier=1).then_inc(masks_made, 1)
                for u in range(2):
                    pool.affine_select(out=first[:, u, :], in_=first[:, u, :], compare_op=ALU.is_gt, fill=0.0,
                                       base=u * P, pattern=[[-1, 2 * P]], channel_multiplier=1).then_inc(masks_made, 1)
                for u in range(2):
                    pool.iota(dumpi[:, u:G:2], pattern=[[0, G // 2]], base=DUMP + u, channel_multiplier=TILES).then_inc(masks_made, 1)

                def gather(g, s, j):
                    if j == 0:
                        pool.wait_ge(gidx_made, g + 1)
                        pool.wait_ge(h_made, two_back(g))
                        settle_waits(pool, pool_mark)
                    pool.indirect_dma_start(out=xs[:, s, j, :], out_offset=None, in_=xrows,
                                            in_offset=bass.IndirectOffsetOnAxis(ap=gidx[:, s, j:j + 1], axis=0)).then_inc(xs_in[s], 16)

                def scatter(g, s, j):
                    if j == 0:
                        pool.wait_ge(tot_out, done(g))
                        pool.wait_ge(sidx_copied, done(g))
                    if j % 2 == 0:
                        if not (isinstance(g, int) and g == j == 0):
                            for u in range(2):
                                pool.wait_ge(scattered[u], pairs_landed(g, j // 2))
                        settle_waits(pool, pool_mark)
                    pool.indirect_dma_start(out=aggrows, out_offset=bass.IndirectOffsetOnAxis(ap=sidx[:, s, j:j + 1], axis=0),
                                            in_=tot[:, s, j, :], in_offset=None, compute_op=ALU.add,
                                            bounds_check=P * TILES - 1, oob_is_err=True).then_inc(scattered[j % 2], 16)

                for s in range(2):
                    for j in range(G):
                        gather(s, s, j)
                pool.wait_ge(agg0_zeroed, 16 * ZN)

                def group(g, s, ahead):
                    for half in range(2):
                        for j in (2 * half, 2 * half + 1):
                            scatter(g, s, j)
                        for j in (2 * half, 2 * half + 1):
                            if ahead:
                                gather(g + 2, s, j)

                group(0, 0, True)
                group(1, 1, True)
                with pool.Fori(1, EG // 2 - 1) as it:
                    for s in range(2):
                        group(it * 2 + s, s, True)
                group(EG - 3, 0, True)
                group(EG - 2, 1, False)
                group(EG - 1, 0, False)
                for u in range(2):
                    pool.wait_ge(scattered[u], pairs_landed(EG))

            @block.vector
            def _(dve):
                V = nc.vector
                V.memset(eaT[C:C1, :, :], 1.0).then_inc(ones_made, 1)
                dve.wait_ge(idx_in, 32)
                V.memset(srci[:, ET:IDX], 0)
                V.memset(dsti[:, ET:IDX], 0).then_inc(rows_made, 1)
                dve.wait_ge(rows_made, 1)
                n = 1
                for of, to in ((srci, k.src_row), (dsti, k.dst_row)):
                    V.tensor_scalar(lo[:, :], of[:, :], P - 1, None, ALU.bitwise_and).then_inc(rows_made, 1)
                    V.tensor_scalar(hi[:, :], of[:, :], 7, None, ALU.logical_shift_right).then_inc(rows_made, 1)
                    dve.wait_ge(rows_made, n + 2)
                    V.scalar_tensor_tensor(to[:, :], lo[:, :], float(TILES), hi[:, :], ALU.mult, ALU.add).then_inc(rows_made, 1)
                    n += 3
                    dve.wait_ge(rows_made, n)
                V.tensor_copy(k.dst_f[:, :], dsti[:, 0:ET])
                for s in range(2):
                    V.tensor_copy(gidx[:, s, :], k.src_row[:, s * G:(s + 1) * G]).then_inc(gidx_made, 1)
                dve.wait_ge(masks_made, 5)
                V.tensor_copy(dumpf[:, :], dumpi[:, :]).then_inc(rows_made, 1)
                dve.wait_ge(rows_made, n + 1)
                V.tensor_tensor(dump[:, :].rearrange("p (g j) -> p g j", j=G),
                                dumpf[:, :].rearrange("p (o j) -> p o j", o=1).broadcast_to([P, EG, G]),
                                k.dst_row[:, 0:ET].rearrange("p (g j) -> p g j", j=G), ALU.subtract).then_inc(rows_made, 1)
                dve.wait_ge(const_in, 16 * 12)
                V.tensor_scalar(k.one_eps[:, :], k.one_eps[:, :], 1.0, None, ALU.add)
                V.memset(k.ln_eps[:, :], LN_EPS).then_inc(rows_made, 1)
                dve.wait_ge(rows_made, n + 3)

                def group(g, s, turn, cols, again=True):
                    dve.wait_ge(xs_in[s], 16 * G * (turn + 1))
                    dve.wait_ge(x_in[s], landed(turn))
                    for j in range(G):
                        V.bn_stats(bn[:, s, j, :], xs[:, s, j, :])
                    for j in range(2 * G):
                        last = V.bn_stats(bn[:, s, G + j, :], k.R[:, span(g * 2 * G + j, 1), :])
                    last.then_inc(bn_made, 1)
                    V.tensor_copy(gidx[:, s, :], k.src_row[:, tiles(g + 2)]).then_inc(gidx_made, 1)
                    dve.wait_ge(bn_made, done(g))
                    settle_waits(dve, dve_mark)
                    for j in range(3 * G):
                        last = V.bn_aggr(mv[:, s, j, :], bn[:, s, j, :])
                    last.then_inc(mv_made, 1)
                    dve.wait_ge(dr_in[s], landed(turn))
                    dve.wait_ge(tot_made, two_back(g))
                    for j in range(G):
                        pair = dr[:, s, (j // 2) * 2 * P:(j // 2 + 1) * 2 * P]
                        last = V.tensor_scalar(S[:, s, j, :], pair, k.dst_f[:, span(g * G + j, 1)], None, ALU.is_equal)
                    last.then_inc(S_made, 1)
                    for j in range(G):
                        pair = dr[:, s, (j // 2) * 2 * P:(j // 2 + 1) * 2 * P]
                        last = V.scalar_tensor_tensor(junk[:, j, :], pair, k.dst_f[:, span(g * G + j, 1)], first[:, j % 2, :],
                                                      ALU.is_equal, ALU.mult, accum_out=earlier[:, s, j:j + 1])
                    last.then_inc(earlier_made, 1)
                    dve.wait_ge(std_made, done(g))
                    V.reciprocal(rs[:, s, :], sd[:, s, 0:G])
                    V.reciprocal(k.rstd[:, span(g * 2 * G, 2 * G)], sd[:, s, G:3 * G]).then_inc(rs_made, 1)
                    dve.wait_ge(rs_made, done(g))
                    V.scalar_tensor_tensor(k.nbias[:, span(g * 2 * G, 2 * G)], mv[:, s, G:3 * G, 0], -1.0,
                                           k.rstd[:, span(g * 2 * G, 2 * G)], ALU.mult, ALU.mult)
                    V.scalar_tensor_tensor(nb[:, s, :], mv[:, s, 0:G, 0], -1.0, rs[:, s, :], ALU.mult, ALU.mult).then_inc(nb_made, 1)
                    dve.wait_ge(earlier_made, done(g))
                    V.tensor_scalar(dup[:, s, :], earlier[:, s, :], 0.0, None, ALU.is_gt).then_inc(dup_made, 1)
                    dve.wait_ge(efr_made, done(g))
                    V.bn_stats(k.ef_bn[:, span(g, 1), :], efT[:, s, 0:cols]).then_inc(efst_made, 1)
                    dve.wait_ge(dup_made, done(g))
                    V.tensor_tensor(dup[:, s, :], dup[:, s, :], dump[:, tiles(g)], ALU.mult).then_inc(shift_made, 1)
                    dve.wait_ge(h_made, done(g))
                    dve.wait_ge(pre_made, done(g))
                    V.tensor_tensor(h[:, s, :, :], ps_pre[s][:, :, :], h[:, s, :, :], ALU.add).then_inc(sum_made, 1)
                    dve.wait_ge(shift_made, done(g))
                    V.tensor_tensor(k.scatter_row[:, tiles(g)], dup[:, s, :], k.dst_row[:, tiles(g)], ALU.add).then_inc(sidx_made, 1)
                    dve.wait_ge(sidx_made, done(g))
                    if again:
                        for u in range(2):
                            dve.wait_ge(scattered[u], pairs_landed(g - 1))
                        settle_waits(dve, dve_mark)
                    V.tensor_copy(sidx[:, s, :], k.scatter_row[:, tiles(g)]).then_inc(sidx_copied, 1)

                group(0, 0, 0, W, again=False)
                group(1, 1, 0, W, again=False)
                with dve.Fori(1, EG // 2) as it:
                    for s in range(2):
                        group(it * 2 + s, s, it, W)
                group(EG - 1, 0, EG // 2, EW_LAST)

            @block.scalar
            def _(act):
                A = nc.scalar
                act.wait_ge(rows_made, 10)

                def group(g, s, again=True):
                    act.wait_ge(mv_made, done(g))
                    act.wait_ge(nb_made, two_back(g))
                    A.activation(sd[:, s, :], mv[:, s, :, 1], ACT.Sqrt, bias=k.ln_eps[:, :]).then_inc(std_made, 1)
                    act.wait_ge(ef_made, done(g))
                    act.wait_ge(efst_made, two_back(g))
                    A.activation(efT[:, s, :], ps_ef[s][:, :], ACT.Relu, bias=k.b_ef[:, :]).then_inc(efr_made, 1)
                    act.wait_ge(nb_made, done(g))
                    act.wait_ge(msg_made, two_back(g))
                    for j in range(G):
                        last = A.activation(h[:, s, j, :], xs[:, s, j, :], ACT.Relu, bias=nb[:, s, j:j + 1], scale=rs[:, s, j:j + 1])
                    last.then_inc(h_made, 1)
                    act.wait_ge(sum_made, done(g))
                    act.wait_ge(tot_made, two_back(g))
                    A.activation(msg[:, s, :, :], h[:, s, :, :], ACT.Relu).then_inc(msg_made, 1)
                    act.wait_ge(tot_made, done(g))
                    if again:
                        for u in range(2):
                            act.wait_ge(scattered[u], pairs_landed(g - 1))
                    A.copy(tot[:, s, :, :], ps_tot[s][:, :, :]).then_inc(tot_out, 1)

                group(0, 0, again=False)
                group(1, 1, again=False)
                with act.Fori(1, EG // 2) as it:
                    for s in range(2):
                        group(it * 2 + s, s)
                group(EG - 1, 0)

            @block.tensor
            def _(pe):
                T = nc.tensor
                pe.wait_ge(const_in, 16 * 12)
                pe.wait_ge(ones_made, 1)

                def group(g, s, turn):
                    pe.wait_ge(ea_in[s], landed(turn))
                    pe.wait_ge(sum_made, two_back(g))
                    for j in range(G):
                        last = T.matmul(ps_pre[s][:, j, :], eaT[:, s, j * P:(j + 1) * P], k.w_e0[:, :], start=True, stop=True)
                    last.then_inc(pre_made, 1)
                    pe.wait_ge(ea4_in[s], landed(turn))
                    pe.wait_ge(efr_made, two_back(g))
                    T.matmul(ps_ef[s][:, :], k.w_ef[:, :], ea4T[:, s, :], start=True, stop=True).then_inc(ef_made, 1)
                    pe.wait_ge(S_made, done(g))
                    pe.wait_ge(msg_made, done(g))
                    pe.wait_ge(tot_out, two_back(g))
                    for j in range(G):
                        for u in range(2):
                            i = j // 2 * 2 + u
                            last = T.matmul(ps_tot[s][:, j, :], S[:, s, i, (j % 2) * P:(j % 2 + 1) * P], msg[:, s, i, :],
                                            start=(u == 0), stop=(u == 1))
                    last.then_inc(tot_made, 1)

                with pe.Fori(0, EG // 2) as it:
                    for s in range(2):
                        group(it * 2 + s, s, it)
                group(EG - 1, 0, EG // 2)


def node_phase(nc, d, k):
    with Phase(nc, "n0") as ph:
        agg = ph.sb("agg", [P, 2, G, C])
        h0 = ph.sb("h0", [P, 2, G, C])
        hh = ph.sb("hh", [P, 2, G, C])
        hhT = ph.sb("hhT", [C, 2, W])
        r1T = ph.sb("r1T", [C1, 2, W])
        bn = ph.sb("bn", [P, 2, G, 6])
        mv = ph.sb("mean_var", [P, 2, G, 2])
        sd = ph.sb("std", [P, 2, G])
        rs = ph.sb("rstd", [P, 2, G])
        nb = ph.sb("nbias", [P, 2, G])
        h1 = ph.sb("h1", [P, 2, G, C])
        zero = ph.sb("zero", [P, 2 * G, C1])
        efmv = ph.sb("ef_mean_var", [C, 2])
        efsd = ph.sb("ef_std", [C, 1])
        efa = ph.sb("ef_scale", [C, 1])
        fold = ph.sb("ef_fold", [C, C1])
        ps_T = [ph.ps(f"T{s}", [C, W]) for s in range(2)]
        ps_1 = [ph.ps(f"w1{s}", [C, W]) for s in range(2)]
        ps_2 = [ph.ps(f"w2{s}", [P, G, C]) for s in range(2)]
        ps_f = ph.ps("fold", [C1, C])

        setup = ph.sem("setup")
        std_ef, fold_made = ph.sem("std_ef"), ph.sem("fold_made")
        made = ph.sem("made")
        agg_in, h1_out = ph.sems("agg_in"), ph.sems("h1_out")
        agg1_zeroed = ph.sem("agg1_zeroed")
        h0_made, h0_scaled, hh_made = ph.count("h0_made"), ph.count("h0_scaled"), ph.count("hh_made")
        T_made, hhT_made, w1_made, r1_made = (ph.count(n) for n in ("T_made", "hhT_made", "w1_made", "r1_made"))
        w2_made, x1_made, bn_made, mv_made = (ph.count(n) for n in ("w2_made", "x1_made", "bn_made", "mv_made"))
        std_made, rs_made, nb_made, h1_made = (ph.count(n) for n in ("std_made", "rs_made", "nb_made", "h1_made"))
        LAG = 4

        def steps(eng, step):
            first = LAG + LAG % 2
            for t in range(first):
                step(t, t % 2, lambda lag, t=t: 0 <= t - lag)
            with eng.Fori(first // 2, NG // 2) as it:
                for s in range(2):
                    step(it * 2 + s, s, lambda lag: True)
            for t in range(NG, NG + LAG):
                step(t, t % 2, lambda lag, t=t: t - lag < NG)

        pool_mark, dve_mark = ph.sem("pool_mark"), ph.sem("dve_mark")

        with nc.Block() as block:

            @block.sync
            def _(sp):
                def load(g, s):
                    sp.wait_ge(hh_made, two_back(g))
                    sp.dma_start(agg[:, s, :, :], d["agg0"][:, tiles(g), :]).then_inc(agg_in[s], 16)

                sp.wait_ge(made, 2)
                with sp.Fori(0, NG // 2) as it:
                    for s in range(2):
                        load(it * 2 + s, s)
                    sp.dma_start(d["agg1"][:, bass.ds(it * 2 * G, 2 * G), :], zero[:, :, :]).then_inc(agg1_zeroed, 16)
                sp.dma_start(d["agg1"][:, NT:TILES, :], zero[:, 0:TILES - NT, :]).then_inc(agg1_zeroed, 16)
                sp.dma_start(d["h1"][:, NT:TILES, :], zero[:, 0:TILES - NT, 0:C]).then_inc(agg1_zeroed, 16)
                sp.wait_ge(agg1_zeroed, 16 * (NG // 2 + 2))

            @block.gpsimd
            def _(pool):
                ph.prime(pool)
                pool.memset(zero[:, :, :], 0.0).then_inc(made, 1)
                for s in range(2):
                    pool.sem_inc(h1_out[s], 16)

                def group(g, s, turn):
                    pool.wait_ge(h0_made, done(g))
                    settle_waits(pool, pool_mark)
                    pool.tensor_scalar(h0[:, s, :, :], h0[:, s, :, :], k.one_eps[:, :], 0.0, ALU.mult, ALU.add).then_inc(h0_scaled, 1)
                    pool.wait_ge(h0_scaled, done(g))
                    pool.wait_ge(agg_in[s], landed(turn))
                    pool.wait_ge(T_made, two_back(g))
                    pool.tensor_tensor(hh[:, s, :, :], h0[:, s, :, :], agg[:, s, :, :], ALU.add).then_inc(hh_made, 1)

                with pool.Fori(0, NG // 2) as it:
                    for s in range(2):
                        group(it * 2 + s, s, it)

            @block.scalar
            def _(act):
                A = nc.scalar
                act.wait_ge(setup, 1)
                A.activation(efsd[:, :], efmv[:, 1:2], ACT.Sqrt, bias=k.ln_eps[0:C, :]).then_inc(std_ef, 1)

                def step(t, s, live):
                    if live(0):
                        act.wait_ge(hh_made, two_back(t))
                        for j in range(G):
                            last = A.activation(h0[:, s, j, :], k.R[:, span(t * G + j, 1), :], ACT.Relu,
                                                bias=k.nbias[:, span(t * G + j, 1)], scale=k.rstd[:, span(t * G + j, 1)])
                        last.then_inc(h0_made, 1)
                    if live(2):
                        g = t - 2
                        act.wait_ge(w1_made, done(g))
                        act.wait_ge(w2_made, two_back(g))
                        A.activation(r1T[0:C, s, :], ps_1[s][:, :], ACT.Relu, bias=k.b1[:, :]).then_inc(r1_made, 1)
                    if live(3):
                        g, z = t - 3, 1 - s
                        act.wait_ge(mv_made, done(g))
                        act.wait_ge(rs_made, two_back(g))
                        A.activation(sd[:, z, :], mv[:, z, :, 1], ACT.Sqrt, bias=k.ln_eps[:, :]).then_inc(std_made, 1)
                    if live(4):
                        g = t - 4
                        act.wait_ge(nb_made, done(g))
                        if isinstance(t, int):
                            turn = g // 2
                        else:
                            turn = None
                        act.wait_ge(h1_out[s], (g - s) * 8 + 16)
                        for j in range(G):
                            last = A.activation(h1[:, s, j, :], k.R[:, span(g * G + j, 1), :], ACT.Relu,
                                                bias=nb[:, s, j:j + 1], scale=rs[:, s, j:j + 1])
                        last.then_inc(h1_made, 1)
                        act.wait_ge(h1_made, done(g))
                        act.dma_start(d["h1"][:, tiles(g), :], h1[:, s, :, :]).then_inc(h1_out[s], 16)

                steps(act, step)
                for s in range(2):
                    act.wait_ge(h1_out[s], landed(NG // 2))

            @block.vector
            def _(dve):
                V = nc.vector
                V.memset(r1T[C:C1, :, :], 1.0).then_inc(made, 1)
                V.bn_aggr(efmv[:, :], k.ef_bn[:, :, :]).then_inc(setup, 1)
                dve.wait_ge(std_ef, 1)
                V.reciprocal(efa[:, :], efsd[:, :]).then_inc(setup, 1)
                dve.wait_ge(setup, 2)
                V.tensor_tensor(efa[:, :], efa[:, :], k.bn_gb[:, 2:3], ALU.mult).then_inc(setup, 1)
                dve.wait_ge(setup, 3)
                V.tensor_scalar(fold[:, 0:C], k.ident[0:C, 0:C], efa[:, :], None, ALU.mult)
                V.tensor_tensor(fold[:, C:C1], efmv[:, 0:1], efa[:, :], ALU.mult).then_inc(setup, 1)
                dve.wait_ge(setup, 4)
                V.tensor_tensor(fold[:, C:C1], k.bn_gb[:, 3:4], fold[:, C:C1], ALU.subtract).then_inc(setup, 1)
                dve.wait_ge(fold_made, 1)
                V.tensor_copy(k.w_ef_msg[0:C, :], ps_f[0:C, :])
                V.tensor_tensor(k.w_ef_msg[C:C1, :], ps_f[C:C1, :], k.b_msg[C:C1, :], ALU.add)

                def step(t, s, live):
                    z = 1 - s
                    if live(1):
                        g = t - 1
                        dve.wait_ge(T_made, done(g))
                        dve.wait_ge(w1_made, two_back(g))
                        V.tensor_copy(hhT[:, z, :], ps_T[z][:, :]).then_inc(hhT_made, 1)
                    if live(4):
                        g = t - 4
                        dve.wait_ge(std_made, done(g))
                        dve.wait_ge(h1_made, two_back(g))
                        V.reciprocal(rs[:, s, :], sd[:, s, :]).then_inc(rs_made, 1)
                        dve.wait_ge(rs_made, done(g))
                        V.scalar_tensor_tensor(nb[:, s, :], mv[:, s, :, 0], -1.0, rs[:, s, :], ALU.mult, ALU.mult).then_inc(nb_made, 1)
                    if live(3):
                        g = t - 3
                        dve.wait_ge(w2_made, done(g))
                        V.tensor_tensor(k.R[:, tiles(g), :], ps_2[z][:, :, :], k.R[:, tiles(g), :], ALU.add).then_inc(x1_made, 1)
                        dve.wait_ge(x1_made, done(g))
                        settle_waits(dve, dve_mark)
                        for j in range(G):
                            last = V.bn_stats(bn[:, z, j, :], k.R[:, span(g * G + j, 1), :])
                        last.then_inc(bn_made, 1)
                        dve.wait_ge(bn_made, done(g))
                        dve.wait_ge(nb_made, two_back(g))
                        settle_waits(dve, dve_mark)
                        for j in range(G):
                            last = V.bn_aggr(mv[:, z, j, :], bn[:, z, j, :])
                        last.then_inc(mv_made, 1)

                steps(dve, step)

            @block.tensor
            def _(pe):
                T = nc.tensor
                pe.wait_ge(setup, 5)
                T.matmul(ps_f[:, :], fold[:, :], k.w_msg[:, 2, :], start=True, stop=True).then_inc(fold_made, 1)
                pe.wait_ge(made, 2)

                def step(t, s, live):
                    z = 1 - s
                    if live(1):
                        g = t - 1
                        pe.wait_ge(hh_made, done(g))
                        pe.wait_ge(hhT_made, two_back(g))
                        for j in range(G):
                            last = T.transpose(ps_T[z][:, j * P:(j + 1) * P], hh[:, z, j, :], k.ident[:, :])
                        last.then_inc(T_made, 1)
                    if live(2):
                        g = t - 2
                        pe.wait_ge(hhT_made, done(g))
                        pe.wait_ge(r1_made, two_back(g))
                        T.matmul(ps_1[s][:, :], k.w1[:, :], hhT[:, s, :], start=True, stop=True).then_inc(w1_made, 1)
                    if live(3):
                        g = t - 3
                        pe.wait_ge(r1_made, done(g))
                        pe.wait_ge(x1_made, two_back(g))
                        for j in range(G):
                            last = T.matmul(ps_2[z][:, j, :], r1T[:, z, j * P:(j + 1) * P], k.w2[:, :], start=True, stop=True)
                        last.then_inc(w2_made, 1)

                steps(pe, step)


def edge_phase_1(nc, d, k):
    with Phase(nc, "e1") as ph:
        hs = ph.sb("h_src", [P, 2, G, C])
        hd = ph.sb("h_dst", [P, 2, G, C])
        ea4T = ph.sb("ea4T", [CE, 2, W])
        dr = ph.sb("dst_row", [P, 2, W], INT32)
        hsT = ph.sb("h_srcT", [C, W])
        hdT = ph.sb("h_dstT", [C, W])
        efT = ph.sb("efT", [C1, W])
        msg = ph.sb("msg", [P, 2, G, C1])
        S = ph.sb("same_dst", [P, 2, G, 2 * P])
        tot = ph.sb("tot", [P, 2, G, C1])
        gidx = ph.sb("gather_idx", [P, 2, 2, G], INT32)
        sidx = ph.sb("scatter_idx", [P, 2, G], INT32)
        h1 = ph.sb("h1", [P, 2, G, C])
        h1T = ph.sb("h1T", [C, 2, W])
        uT = ph.sb("uT", [C, 2, W])
        nothing = ph.sb("nothing", [P, C1])
        ps_s = ph.ps("sT", [C, W])
        ps_d = ph.ps("dT", [C, W])
        ps_ef = ph.ps("ef", [C, W])
        ps_m = ph.ps("m", [P, G, C])
        ps_tot = ph.ps("tot", [P, G, C1])
        ps_hT = ph.ps("hT", [C, W])
        ps_u = ph.ps("u", [C, W])
        ps_gram = ph.ps("gram", [C, C1])

        ones_made, nothing_made = ph.sem("ones_made"), ph.sem("nothing_made")
        ea4_in, dr_in, hs_in, hd_in, scattered = (ph.sems(n) for n in ("ea4_in", "dr_in", "hs_in", "hd_in", "scattered"))
        h1_in, uT_out = ph.sems("h1_in"), ph.sems("uT_out")
        gidx_made = ph.sem("gidx_made")
        sidx_copied, S_made, sT_out, dT_out = (ph.count(n) for n in ("sidx_copied", "S_made", "sT_out", "dT_out"))
        s_made, d_made, ef_made, ef_out = (ph.count(n) for n in ("s_made", "d_made", "ef_made", "ef_out"))
        m_made, msg_made, tot_made, tot_out = (ph.count(n) for n in ("m_made", "msg_made", "tot_made", "tot_out"))
        hT_made, hT_out, u_made, uT_made, ubn_made = (ph.count(n) for n in ("hT_made", "hT_out", "u_made", "uT_made", "ubn_made"))
        gram_made = ph.sem("gram_made")

        hrows = d["h1"].rearrange("p t c -> (p t) c")
        aggrows = d["agg1"].rearrange("p t c -> (p t) c")

        pool_mark, dve_mark = ph.sem("pool_mark"), ph.sem("dve_mark")

        with nc.Block() as block:

            @block.sync
            def _(sp):
                def loads(g, s):
                    sp.wait_ge(ef_made, two_back(g))
                    sp.dma_start(ea4T[:, s, :], d["ea4T"][:, span(g * W, W)]).then_inc(ea4_in[s], 16)
                    sp.wait_ge(S_made, two_back(g))
                    sp.dma_start(dr[:, s, :], d["dst_row"][:, span(g * W, W)].broadcast_to([P, W])).then_inc(dr_in[s], 16)
                    for v in range(2):
                        u = g * 2 + v
                        sp.wait_ge(hT_made, two_back(u))
                        sp.dma_start(h1[:, v, :, :], d["h1"][:, tiles(u), :]).then_inc(h1_in[v], 16)

                def stores(g):
                    for v in range(2):
                        u = g * 2 + v
                        sp.wait_ge(uT_made, done(u))
                        sp.dma_start(d["uT"][:, span(u * W, W)], uT[:, v, :]).then_inc(uT_out[v], 16)

                loads(0, 0)
                with sp.Fori(0, EG // 2) as it:
                    for s in range(2):
                        loads(it * 2 + s + 1, 1 - s)
                        stores(it * 2 + s)
                stores(EG - 1)
                for v in range(2):
                    sp.wait_ge(uT_out[v], landed(EG))

            @block.gpsimd
            def _(pool):
                ph.prime(pool)
                pool.memset(msg[:, :, :, C:C1], 1.0).then_inc(ones_made, 1)
                pool.memset(nothing[:, :], 0.0).then_inc(nothing_made, 1)
                for v in range(2):
                    pool.sem_inc(uT_out[v], 16)

                def gather(g, s, j):
                    if j == 0:
                        pool.wait_ge(gidx_made, g + 1)
                        pool.wait_ge(s_made, two_back(g))
                        pool.wait_ge(d_made, two_back(g))
                        settle_waits(pool, pool_mark)
                    for v, (to, got) in enumerate(((hs, hs_in), (hd, hd_in))):
                        pool.indirect_dma_start(out=to[:, s, j, :], out_offset=None, in_=hrows,
                                                in_offset=bass.IndirectOffsetOnAxis(ap=gidx[:, s, v, j:j + 1], axis=0)).then_inc(got[s], 16)

                def scatter(g, s, j):
                    if j == 0:
                        pool.wait_ge(tot_out, done(g))
                        pool.wait_ge(sidx_copied, done(g))
                    if j % 2 == 0:
                        if not (isinstance(g, int) and g == j == 0):
                            for u in range(2):
                                pool.wait_ge(scattered[u], pairs_landed(g, j // 2))
                        settle_waits(pool, pool_mark)
                    pool.indirect_dma_start(out=aggrows, out_offset=bass.IndirectOffsetOnAxis(ap=sidx[:, s, j:j + 1], axis=0),
                                            in_=tot[:, s, j, :], in_offset=None, compute_op=ALU.add,
                                            bounds_check=P * TILES - 1, oob_is_err=True).then_inc(scattered[j % 2], 16)

                for s in range(2):
                    for j in range(G):
                        gather(s, s, j)

                def group(g, s, ahead):
                    for half in range(2):
                        for j in (2 * half, 2 * half + 1):
                            scatter(g, s, j)
                        for j in (2 * half, 2 * half + 1):
                            if ahead:
                                gather(g + 2, s, j)

                group(0, 0, True)
                group(1, 1, True)
                with pool.Fori(1, EG // 2 - 1) as it:
                    for s in range(2):
                        group(it * 2 + s, s, True)
                group(EG - 3, 0, True)
                group(EG - 2, 1, False)
                group(EG - 1, 0, False)
                for u in range(2):
                    pool.wait_ge(scattered[u], pairs_landed(EG))

            @block.vector
            def _(dve):
                V = nc.vector
                V.memset(efT[C:C1, :], 1.0).then_inc(ones_made, 1)

                def indices(g, s):
                    V.tensor_copy(gidx[:, s, 0, :], k.src_row[:, tiles(g)])
                    V.tensor_copy(gidx[:, s, 1, :], k.dst_row[:, tiles(g)]).then_inc(gidx_made, 1)

                for s in range(2):
                    indices(s, s)

                def group(g, s, turn, cols, again=True):
                    dve.wait_ge(dr_in[s], landed(turn))
                    dve.wait_ge(tot_made, two_back(g))
                    for j in range(G):
                        pair = dr[:, s, (j // 2) * 2 * P:(j // 2 + 1) * 2 * P]
                        last = V.tensor_scalar(S[:, s, j, :], pair, k.dst_f[:, span(g * G + j, 1)], None, ALU.is_equal)
                    last.then_inc(S_made, 1)
                    dve.wait_ge(d_made, done(g))
                    dve.wait_ge(m_made, one_back(g))
                    V.tensor_copy(hdT[:, :], ps_d[:, :]).then_inc(dT_out, 1)
                    dve.wait_ge(hs_in[s], 16 * G * (turn + 1))
                    dve.wait_ge(hd_in[s], 16 * G * (turn + 1))
                    indices(g + 2, s)
                    if again:
                        for u in range(2):
                            dve.wait_ge(scattered[u], pairs_landed(g - 1))
                        settle_waits(dve, dve_mark)
                    V.tensor_copy(sidx[:, s, :], k.scatter_row[:, tiles(g)]).then_inc(sidx_copied, 1)
                    for v in range(2):
                        u = g * 2 + v
                        dve.wait_ge(hT_made, done(u))
                        dve.wait_ge(u_made, two_back(u))
                        V.tensor_copy(h1T[:, v, :], ps_hT[:, :]).then_inc(hT_out, 1)
                    for v in range(2):
                        u = g * 2 + v
                        dve.wait_ge(uT_made, done(u))
                        settle_waits(dve, dve_mark)
                        V.bn_stats(k.u_bn[:, span(u, 1), :], uT[:, v, 0:cols if v else W]).then_inc(ubn_made, 1)

                group(0, 0, 0, W, again=False)
                group(1, 1, 0, W, again=False)
                with dve.Fori(1, EG // 2) as it:
                    for s in range(2):
                        group(it * 2 + s, s, it, W)
                group(EG - 1, 0, EG // 2, NW_LAST)
                dve.wait_ge(gram_made, 1)
                V.tensor_copy(k.gram[:, :], ps_gram[:, :])

            @block.scalar
            def _(act):
                A = nc.scalar

                def group(g, s, again=True):
                    act.wait_ge(s_made, done(g))
                    act.wait_ge(m_made, one_back(g))
                    A.copy(hsT[:, :], ps_s[:, :]).then_inc(sT_out, 1)
                    act.wait_ge(ef_made, done(g))
                    A.activation(efT[0:C, :], ps_ef[:, :], ACT.Relu, bias=k.b_ef[:, :]).then_inc(ef_out, 1)
                    act.wait_ge(m_made, done(g))
                    act.wait_ge(tot_made, two_back(g))
                    A.activation(msg[:, s, :, 0:C], ps_m[:, :, :], ACT.Relu).then_inc(msg_made, 1)
                    for v in range(2):
                        u = g * 2 + v
                        if v == 1:
                            act.wait_ge(tot_made, done(g))
                            if again:
                                for w in range(2):
                                    act.wait_ge(scattered[w], pairs_landed(g - 1))
                            A.copy(tot[:, s, :, :], ps_tot[:, :, :]).then_inc(tot_out, 1)
                        act.wait_ge(u_made, done(u))
                        act.wait_ge(ubn_made, two_back(u))
                        act.wait_ge(uT_out[v], landed(g))
                        A.activation(uT[:, v, :], ps_u[:, :], ACT.Relu, bias=k.b_node[:, :]).then_inc(uT_made, 1)

                group(0, 0, again=False)
                group(1, 1, again=False)
                with act.Fori(1, EG // 2) as it:
                    for s in range(2):
                        group(it * 2 + s, s)
                group(EG - 1, 0)

            @block.tensor
            def _(pe):
                T = nc.tensor
                pe.wait_ge(nothing_made, 1)
                pe.wait_ge(ones_made, 2)
                T.matmul(ps_gram[:, :], nothing[:, 0:C], nothing[:, :], start=True, stop=False)

                def transposes(to, of, s, made):
                    for j in range(G):
                        last = T.transpose(to[:, j * P:(j + 1) * P], of[:, s, j, :], k.ident[:, :])
                    last.then_inc(made, 1)

                def node_T(u, v, turn):
                    pe.wait_ge(h1_in[v], landed(turn))
                    pe.wait_ge(hT_out, one_back(u))
                    transposes(ps_hT, h1, v, hT_made)

                def node_mm(u, v):
                    pe.wait_ge(hT_out, done(u))
                    pe.wait_ge(uT_made, one_back(u))
                    T.matmul(ps_u[:, :], k.w_node[:, :], h1T[:, v, :], start=True, stop=True).then_inc(u_made, 1)

                def group(g, s, turn, last_rows=P):
                    pe.wait_ge(hs_in[s], 16 * G * (turn + 1))
                    pe.wait_ge(sT_out, one_back(g))
                    transposes(ps_s, hs, s, s_made)
                    pe.wait_ge(hd_in[s], 16 * G * (turn + 1))
                    pe.wait_ge(dT_out, one_back(g))
                    transposes(ps_d, hd, s, d_made)
                    pe.wait_ge(ea4_in[s], landed(turn))
                    pe.wait_ge(ef_out, one_back(g))
                    T.matmul(ps_ef[:, :], k.w_ef[:, :], ea4T[:, s, :], start=True, stop=True).then_inc(ef_made, 1)
                    node_T(g * 2, 0, g)
                    pe.wait_ge(sT_out, done(g))
                    pe.wait_ge(dT_out, done(g))
                    pe.wait_ge(ef_out, done(g))
                    pe.wait_ge(msg_made, one_back(g))
                    for j in range(G):
                        for n, (x, w) in enumerate(((hsT, k.w_msg[:, 0, :]), (hdT, k.w_msg[:, 1, :]), (efT, k.w_ef_msg[:, :]))):
                            last = T.matmul(ps_m[:, j, :], x[:, j * P:(j + 1) * P], w, start=(n == 0), stop=(n == 2))
                    last.then_inc(m_made, 1)
                    node_mm(g * 2, 0)
                    node_T(g * 2 + 1, 1, g)
                    pe.wait_ge(S_made, done(g))
                    pe.wait_ge(msg_made, done(g))
                    pe.wait_ge(tot_out, one_back(g))
                    for j in range(G):
                        r = last_rows if j == G - 1 else P
                        last = T.matmul(ps_gram[:, :], msg[0:r, s, j, 0:C], msg[0:r, s, j, :], start=False, stop=(r < P))
                    if last_rows < P:
                        last.then_inc(gram_made, 1)
                    for j in range(G):
                        for u in range(2):
                            i = j // 2 * 2 + u
                            last = T.matmul(ps_tot[:, j, :], S[:, s, i, (j % 2) * P:(j % 2 + 1) * P], msg[:, s, i, :],
                                            start=(u == 0), stop=(u == 1))
                    last.then_inc(tot_made, 1)
                    node_mm(g * 2 + 1, 1)

                with pe.Fori(0, EG // 2) as it:
                    for s in range(2):
                        group(it * 2 + s, s, it)
                group(EG - 1, 0, EG // 2, EDGES_LAST)


def final_phase(nc, d, k):
    with Phase(nc, "f") as ph:
        agg = ph.sb("agg", [P, 2, G, C1])
        uT = ph.sb("uT", [C1, 2, W])
        aggT = ph.sb("aggT", [C1, 2, W])
        y = ph.sb("y", [P, 2, G, C])
        st = ph.sb("stats", [C, 2, 2])
        tmp = ph.sb("tmp", [C, C])
        sd = ph.sb("std", [C, 2])
        scale = ph.sb("scale", [C, 2])
        fold = ph.sb("fold", [C, 2, C1])
        w = ph.sb("w_out", [C1, 2, C])
        ps_f = ph.ps("fold", [C1, 2, C])
        ps_T = [ph.ps(f"T{s}", [C1, W]) for s in range(2)]
        ps_y = [ph.ps(f"y{s}", [P, G, C]) for s in range(2)]

        made, setup, std_made, fold_made = (ph.sem(n) for n in ("made", "setup", "std_made", "fold_made"))
        agg_in, uT_in, y_out = ph.sems("agg_in"), ph.sems("uT_in"), ph.sems("y_out")
        T_made, T_out, ps_made, y_made = (ph.count(n) for n in ("T_made", "T_out", "ps_made", "y_made"))
        SETUP = 8

        def groups(eng, group, lag=0):
            with eng.Fori(0, NG // 2) as it:
                for s in range(2):
                    group(it * 2 + s, s, it)

        pool_mark, dve_mark = ph.sem("pool_mark"), ph.sem("dve_mark")

        with nc.Block() as block:

            @block.sync
            def _(sp):
                def load(g, s):
                    sp.wait_ge(T_made, two_back(g))
                    sp.dma_start(agg[:, s, :, :], d["agg1"][:, tiles(g), :]).then_inc(agg_in[s], 16)
                    sp.wait_ge(ps_made, two_back(g))
                    sp.dma_start(uT[0:C, s, :], d["uT"][:, span(g * W, W)]).then_inc(uT_in[s], 16)

                def store(g, s):
                    sp.wait_ge(y_made, done(g))
                    sp.dma_start(d["out"][:, tiles(g), :], y[:, s, :, :]).then_inc(y_out[s], 16)

                load(0, 0)
                load(1, 1)
                with sp.Fori(1, NG // 2) as it:
                    for s in range(2):
                        load(it * 2 + s, s)
                        store(it * 2 + s - 2, s)
                for s in range(2):
                    store(NG - 2 + s, s)
                for s in range(2):
                    sp.wait_ge(y_out[s], landed(NG // 2))

            @block.gpsimd
            def _(pool):
                ph.prime(pool)
                for s in range(2):
                    pool.sem_inc(y_out[s], 16)

            @block.vector
            def _(dve):
                V = nc.vector
                V.memset(uT[C:C1, :, :], 1.0).then_inc(made, 1)
                n = 0

                def settle(ins):
                    nonlocal n
                    n += 1
                    ins.then_inc(setup, 1)
                    dve.wait_ge(setup, n)

                V.bn_aggr(st[:, 0, :], k.u_bn[:, :, :])
                V.tensor_scalar(st[:, 1, 0:1], k.gram[:, C:C1], 1.0 / EDGES, None, ALU.mult)
                settle(V.tensor_tensor(tmp[:, :], k.gram[:, 0:C], k.ident[0:C, 0:C], ALU.mult))
                settle(V.reduce_sum(st[:, 1, 1:2], tmp[:, :], AX.X))
                settle(V.tensor_tensor(sd[:, 1:2], st[:, 1, 0:1], st[:, 1, 0:1], ALU.mult))
                settle(V.scalar_tensor_tensor(st[:, 1, 1:2], st[:, 1, 1:2], 1.0 / EDGES, sd[:, 1:2], ALU.mult, ALU.subtract))
                dve.wait_ge(std_made, 1)
                settle(V.reciprocal(scale[:, :], sd[:, :]))
                settle(V.tensor_tensor(scale[:, :], scale[:, :], k.bn_gb[:, 0:5:4], ALU.mult))
                for i in range(2):
                    V.tensor_scalar(fold[:, i, 0:C], k.ident[0:C, 0:C], scale[:, i:i + 1], None, ALU.mult)
                settle(V.tensor_tensor(fold[:, :, C], st[:, :, 0], scale[:, :], ALU.mult))
                settle(V.tensor_tensor(fold[:, :, C], k.bn_gb[:, 1:6:4], fold[:, :, C], ALU.subtract))
                assert n == SETUP
                dve.wait_ge(fold_made, 1)
                settle(V.tensor_copy(w[:, :, :], ps_f[:, :, :]))

                def group(g, s, turn):
                    dve.wait_ge(ps_made, done(g))
                    dve.wait_ge(y_out[s], landed(turn))
                    V.tensor_tensor(y[:, s, :, :], ps_y[s][:, :, :], k.R[:, tiles(g), :], ALU.add).then_inc(y_made, 1)

                groups(dve, group)

            @block.scalar
            def _(act):
                A = nc.scalar
                act.wait_ge(setup, 4)
                A.activation(sd[:, :], st[:, :, 1], ACT.Sqrt, bias=k.ln_eps[0:C, :]).then_inc(std_made, 1)

                def group(g, s, turn):
                    act.wait_ge(T_made, done(g))
                    act.wait_ge(ps_made, two_back(g))
                    A.copy(aggT[:, s, :], ps_T[s][:, :]).then_inc(T_out, 1)

                groups(act, group)

            @block.tensor
            def _(pe):
                T = nc.tensor
                pe.wait_ge(setup, SETUP)
                for i in range(2):
                    last = T.matmul(ps_f[:, i, :], fold[:, i, :], k.ident[0:C, 0:C], start=True, stop=True)
                last.then_inc(fold_made, 1)
                pe.wait_ge(made, 1)
                pe.wait_ge(setup, SETUP + 1)

                def transposes(g, s, turn):
                    pe.wait_ge(agg_in[s], landed(turn))
                    pe.wait_ge(T_out, two_back(g))
                    for j in range(G):
                        last = T.transpose(ps_T[s][:, j * P:(j + 1) * P], agg[:, s, j, :], k.ident[:, :])
                    last.then_inc(T_made, 1)

                def sums(g, s, turn):
                    pe.wait_ge(uT_in[s], landed(turn))
                    pe.wait_ge(T_out, done(g))
                    pe.wait_ge(y_made, two_back(g))
                    for j in range(G):
                        T.matmul(ps_y[s][:, j, :], uT[:, s, j * P:(j + 1) * P], w[:, 0, :], start=True, stop=False)
                        last = T.matmul(ps_y[s][:, j, :], aggT[:, s, j * P:(j + 1) * P], w[:, 1, :], start=False, stop=True)
                    last.then_inc(ps_made, 1)

                transposes(0, 0, 0)
                transposes(1, 1, 0)
                sums(0, 0, 0)
                with pe.Fori(1, NG // 2) as it:
                    transposes(it * 2, 0, it)
                    sums(it * 2 - 1, 1, it - 1)
                    transposes(it * 2 + 1, 1, it)
                    sums(it * 2, 0, it)
                sums(NG - 1, 1, NG // 2 - 1)


def gnn_kernel(nc, d):
    with Phase(nc, "all") as ph:
        k = Kept()
        k.R = ph.sb("x", [P, NT, C])
        k.rstd = ph.sb("rstd", [P, NT])
        k.nbias = ph.sb("nbias", [P, NT])
        k.src_row = ph.sb("src_row", [P, IDX], INT32)
        k.dst_row = ph.sb("dst_row", [P, IDX], INT32)
        k.dst_f = ph.sb("dst_f", [P, ET])
        k.scatter_row = ph.sb("scatter_row", [P, ET], INT32)
        k.ident = ph.sb("ident", [P, P])
        k.ln_eps = ph.sb("ln_eps", [P, 1])
        k.one_eps = ph.sb("one_eps", [P, 1])
        k.w_e0 = ph.sb("w_e0", [C1, C])
        k.w_ef = ph.sb("w_ef", [CE, C])
        k.b_ef = ph.sb("b_ef", [C, 1])
        k.w1 = ph.sb("w1", [C, C])
        k.b1 = ph.sb("b1", [C, 1])
        k.w2 = ph.sb("w2", [C1, C])
        k.w_node = ph.sb("w_node", [C, C])
        k.b_node = ph.sb("b_node", [C, 1])
        k.w_msg = ph.sb("w_msg", [C, 3, C])
        k.b_msg = ph.sb("b_msg", [C1, C])
        k.w_ef_msg = ph.sb("w_ef_msg", [C1, C])
        k.bn_gb = ph.sb("bn_gb", [C, 6])
        k.ef_bn = ph.sb("ef_bn", [C, EG, 6])
        k.u_bn = ph.sb("u_bn", [C, NG, 6])
        k.gram = ph.sb("gram", [C, C1])
        edge_phase_0(nc, d, k)
        node_phase(nc, d, k)
        edge_phase_1(nc, d, k)
        final_phase(nc, d, k)


def kernel(x, src, dst, edge_attr_4, edge_attr_96, L0_gnn_W_edge, L0_gnn_b_edge, L0_gnn_eps, L0_gnn_W1, L0_gnn_b1,
           L0_gnn_W2, L0_gnn_b2, L1_gnn_W_node, L1_gnn_b_node, L1_gnn_g_node, L1_gnn_beta_node, L1_gnn_W_edge,
           L1_gnn_b_edge, L1_gnn_g_edge, L1_gnn_beta_edge, L1_gnn_W_msg, L1_gnn_b_msg, L1_gnn_g_msg, L1_gnn_beta_msg):
    import numpy as np
    from concourse import bacc
    from concourse.bass_utils import run_bass_kernel_spmd

    def table(a):
        padded = np.zeros((TILES * P, a.shape[1]), a.dtype)
        padded[:a.shape[0]] = a
        return np.ascontiguousarray(padded.reshape(TILES, P, -1).transpose(1, 0, 2))

    def edges(a, fill):
        padded = np.full(ET * P, fill, np.int32)
        padded[:EDGES] = a
        return padded

    def transposed(a):
        padded = np.zeros((a.shape[1], ET * P), a.dtype)
        padded[:, :EDGES] = np.asarray(a).T
        return padded

    def column(a):
        return np.asarray(a).reshape(-1, 1)

    x, src, dst = np.asarray(x), np.asarray(src), np.asarray(dst)
    src_p, dst_p = edges(src, 0), edges(dst, DUMP * P)
    arrays = {
        "x": table(x),
        "src_col": src_p.reshape(ET, P).T, "dst_col": dst_p.reshape(ET, P).T, "dst_row": dst_p.reshape(1, -1),
        "eaT": transposed(edge_attr_96), "ea4T": transposed(edge_attr_4),
        "w_e0": np.concatenate([np.asarray(L0_gnn_W_edge).T, np.asarray(L0_gnn_b_edge)[None]]),
        "eps": np.asarray(L0_gnn_eps).reshape(1, 1),
        "w1": np.asarray(L0_gnn_W1).T, "b1": column(L0_gnn_b1),
        "w2": np.concatenate([np.asarray(L0_gnn_W2).T, np.asarray(L0_gnn_b2)[None]]),
        "w_node": np.asarray(L1_gnn_W_node), "b_node": column(L1_gnn_b_node),
        "w_ef": np.asarray(L1_gnn_W_edge), "b_ef": column(L1_gnn_b_edge),
        "w_msg": np.asarray(L1_gnn_W_msg).reshape(3, C, C), "b_msg": np.asarray(L1_gnn_b_msg).reshape(1, C),
        "bn_gb": np.concatenate([column(a) for a in (L1_gnn_g_node, L1_gnn_beta_node, L1_gnn_g_edge, L1_gnn_beta_edge,
                                                     L1_gnn_g_msg, L1_gnn_beta_msg)], axis=1),
    }
    arrays = {n: np.ascontiguousarray(a) for n, a in arrays.items()}

    nc = bacc.Bacc("TRN2", target_bir_lowering=False, num_devices=1, dynamic_dma_scratch_size=4096)
    d = {n: nc.dram_tensor(f"in_{n}", a.shape, mybir.dt.from_np(a.dtype), kind="ExternalInput").ap()
         for n, a in arrays.items()}
    d["agg0"] = nc.dram_tensor("agg0", (P, TILES, C), FP32, kind="Internal").ap()
    d["agg1"] = nc.dram_tensor("agg1", (P, TILES, C1), FP32, kind="Internal").ap()
    d["h1"] = nc.dram_tensor("h1", (P, TILES, C), FP32, kind="Internal").ap()
    d["uT"] = nc.dram_tensor("uT", (C, NT * P), FP32, kind="Internal").ap()
    d["out"] = nc.dram_tensor("out", (P, NT, C), FP32, kind="ExternalOutput").ap()
    gnn_kernel(nc, d)
    got = run_bass_kernel_spmd(nc, [{f"in_{n}": a for n, a in arrays.items()}], core_ids=[0]).results[0]["out"]
    return np.asarray(got).transpose(1, 0, 2).reshape(NT * P, C)[:NODES]
```

```python
from contextlib import ExitStack

import concourse.bass as bass
from concourse import mybir

FP32 = mybir.dt.float32
BF16 = mybir.dt.bfloat16
INT32 = mybir.dt.int32
ALU = mybir.AluOpType
ACT = mybir.ActivationFunctionType
AX = mybir.AxisListType

P = 128
NODES, EDGES, C, CE = 50000, 25000, 96, 4
LN_EPS = BN_EPS = 1e-5
G = 4
W = G * P
NT = -(-NODES // W) * G
NG = NT // G
ET = -(-EDGES // P)
EG = ET // G
TILES = NT + 1
DUMP = NT - 1
EDGES_LAST = EDGES - (ET - 1) * P
EW_LAST = EDGES - (EG - 1) * W
NW_LAST = NODES - (NG - 1) * W
assert ET % G == 0 and G == 4 and DUMP * P >= NODES and NG == 2 * EG
C1 = C + 1
DEGREE, ONES, UROWS = C, C + 1, C + 2
ZN = 72
ZW = TILES * C1 // ZN

START = 4


def done(g):
    return g + 1 + START


def ago(g, n):
    return g + 1 + START - n


def landed(turn):
    return 16 * (turn + 1)


def pairs_landed(g, pair=0):
    return 16 * (g * 2 + pair)


class Step:

    def __init__(self, it, pos, unroll, count=None):
        self.it, self.pos, self.unroll, self.count = it, pos, unroll, count

    def group(self, lag):
        return self.it * self.unroll + (self.pos - lag)

    def slot(self, lag, depth=2):
        return (self.pos - lag) % depth

    def turn(self, lag, depth=2):
        return self.it * (self.unroll // depth) + (self.pos - lag) // depth

    def live(self, lag):
        return self.count is None or 0 <= self.group(lag) < self.count

    def last(self, lag):
        return self.count is not None and self.group(lag) == self.count - 1

    def again(self, lag, n=2):
        return self.count is None or self.group(lag) >= n


def run_steps(eng, count, lag, step, unroll):
    first, last = lag // unroll + 1, count // unroll
    for t in range(first * unroll):
        step(Step(t // unroll, t % unroll, unroll, count))
    with eng.Fori(first, last) as it:
        for pos in range(unroll):
            step(Step(it, pos, unroll))
    for t in range(last * unroll, count + lag):
        step(Step(t // unroll, t % unroll, unroll, count))


def settle_waits(eng, mark):
    eng.sem_inc(mark, 1)


class Phase:

    def __init__(self, nc, name):
        self.nc, self.name, self.stack = nc, name, ExitStack()
        self.counts = []

    def __enter__(self):
        self.stack.__enter__()
        return self

    def __exit__(self, *a):
        return self.stack.__exit__(*a)

    def sb(self, name, shape, dt=FP32):
        return self.stack.enter_context(self.nc.sbuf_tensor(f"{self.name}_{name}", shape, dt))

    def ps(self, name, shape, dt=FP32):
        return self.stack.enter_context(self.nc.psum_tensor(f"{self.name}_ps_{name}", shape, dt))

    def sem(self, name):
        return self.stack.enter_context(self.nc.semaphore(f"{self.name}_{name}"))

    def sems(self, name, n=2):
        return [self.sem(f"{name}{i}") for i in range(n)]

    def count(self, name):
        s = self.sem(name)
        self.counts.append(s)
        return s

    def prime(self, eng):
        for s in self.counts:
            eng.sem_inc(s, START)


class Kept:
    pass


def span(start, n):
    return slice(start, start + n) if isinstance(start, int) else bass.ds(start, n)


def tiles(g, n=G):
    return span(g * G, n)


def per_tile(a):
    return a.rearrange("p (t o) -> p t o", o=1).broadcast_to([P, a.shape[1], C])


def edge_phase_0(nc, d, k):
    with Phase(nc, "e0") as ph:
        xs = ph.sb("xs", [P, 4, G, C])
        eaT = ph.sb("eaT", [C1, 2, W])
        ea4T = ph.sb("ea4T", [CE, 2, W])
        dr = ph.sb("dst_row", [P, 2, W], INT32)
        h = ph.sb("h", [P, 2, G, C])
        msg = ph.sb("msg", [P, 2, G, C1])
        efT = ph.sb("efT", [C, 2, W])
        S = ph.sb("same_dst", [P, 2, G, 2 * P])
        tot = ph.sb("tot", [P, 2, G, C1])
        junk = ph.sb("junk", [P, G, 2 * P], BF16)
        first = ph.sb("first_mask", [P, 2, 2 * P])
        bn = ph.sb("bn", [P, 2, 3 * G, 2, 3])
        mean2 = ph.sb("mean2", [P, 2, 3 * G])
        dif = ph.sb("dif", [P, 2, 3 * G])
        sq = ph.sb("squares", [P, 2, 3 * G])
        dif2 = ph.sb("dif2", [P, 2, 3 * G])
        var4 = ph.sb("var4", [P, 2, 3 * G])
        sd = ph.sb("std", [P, 2, 3 * G])
        rs = ph.sb("rstd", [P, 2, 3 * G])
        nb = ph.sb("nbias", [P, 2, G])
        earlier = ph.sb("earlier", [P, 2, G])
        dup = ph.sb("dup", [P, 2, G])
        shift = ph.sb("shift", [P, 2, G])
        srci = ph.sb("src_i", [P, ET], INT32)
        dsti = ph.sb("dst_i", [P, ET], INT32)
        lo = ph.sb("lo", [P, ET], INT32)
        hi = ph.sb("hi", [P, ET], INT32)
        dump = ph.sb("dump_less_row", [P, ET])
        dumpi = ph.sb("dump_i", [P, G], INT32)
        dumpf = ph.sb("dump_f", [P, G])
        gidx = ph.sb("gather_idx", [P, 4, G], INT32)
        sidx = ph.sb("scatter_idx", [P, 2, G], INT32)
        zero = ph.sb("zero", [P, ZW])
        ps_pre = [ph.ps(f"pre{s}", [P, G, C]) for s in range(2)]
        ps_tot = [ph.ps(f"tot{s}", [P, G, C1]) for s in range(2)]
        ps_ef = [ph.ps(f"ef{s}", [C, W]) for s in range(2)]

        const_in, idx_in = ph.sem("const_in"), ph.sem("idx_in")
        zero_made, agg0_zeroed = ph.sem("zero_made"), ph.sem("agg0_zeroed")
        masks_made, masks_filled = ph.sem("masks_made"), ph.sem("masks_filled")
        rows_made, ones_made = ph.sem("rows_made"), ph.sem("ones_made")
        ea_in, ea4_in, dr_in, x_in = (ph.sems(n) for n in ("ea_in", "ea4_in", "dr_in", "x_in"))
        xs_in, scattered = ph.sems("xs_in", 4), ph.sems("scattered")
        gidx_made = ph.count("gidx_made")
        bn_made, halves_made, dif2_made, var_made = (ph.count(n) for n in ("bn_made", "halves_made", "dif2_made", "var_made"))
        std_made, rs_made, nb_made = ph.count("std_made"), ph.count("rs_made"), ph.count("nb_made")
        h_made, msg_made = ph.count("h_made"), ph.count("msg_made")
        S_made, earlier_made, dup_made = ph.count("S_made"), ph.count("earlier_made"), ph.count("dup_made")
        shift_made, srow_made, sidx_made = ph.count("shift_made"), ph.count("srow_made"), ph.count("sidx_made")
        pre_made, ef_made, tot_made = ph.count("pre_made"), ph.count("ef_made"), ph.count("tot_made")
        efr_made, efst_made, tot_out = ph.count("efr_made"), ph.count("efst_made"), ph.count("tot_out")
        pool_mark, dve_mark = ph.sem("pool_mark"), ph.sem("dve_mark")

        xrows = d["x"].rearrange("p t c -> (p t) c")
        aggrows = d["agg0"].rearrange("p t c -> (p t) c")
        LAG = 4

        def steps(eng, step):
            run_steps(eng, EG, LAG, step, 4)

        with nc.Block() as block:

            @block.sync
            def _(sp):
                sp.dma_start(srci[:, :], d["src_col"]).then_inc(idx_in, 16)
                sp.dma_start(dsti[:, :], d["dst_col"]).then_inc(idx_in, 16)
                for to, of in ((k.w_e0[:, :], d["w_e0"]), (k.w_ef[:, :], d["w_ef"]), (k.b_ef[:, :], d["b_ef"]),
                               (k.one_eps[:, :], d["eps"].broadcast_to([P, 1])),
                               (k.w1[:, :], d["w1"]), (k.b1[:, :], d["b1"]), (k.w2[:, :], d["w2"]),
                               (k.w_node[:, :], d["w_node"]), (k.b_node[:, :], d["b_node"]),
                               (k.w_msg[:, :, :], d["w_msg"].rearrange("a i o -> i a o")),
                               (k.b_msg[C:C1, :], d["b_msg"]), (k.bn_gb[:, :], d["bn_gb"])):
                    sp.dma_start(to, of).then_inc(const_in, 16)

                def step(t):
                    if not t.live(0):
                        return
                    g, s = t.group(0), t.slot(0)
                    sp.wait_ge(pre_made, ago(g, 2))
                    sp.dma_start(eaT[0:C, s, :], d["eaT"][:, span(g * W, W)]).then_inc(ea_in[s], 16)
                    sp.wait_ge(ef_made, ago(g, 2))
                    sp.dma_start(ea4T[:, s, :], d["ea4T"][:, span(g * W, W)]).then_inc(ea4_in[s], 16)
                    sp.wait_ge(earlier_made, ago(g, 2))
                    sp.dma_start(dr[:, s, :], d["dst_row"][:, span(g * W, W)].broadcast_to([P, W])).then_inc(dr_in[s], 16)
                    sp.wait_ge(bn_made, ago(g, 2))
                    sp.dma_start(k.R[:, span(g * 2 * G, 2 * G), :], d["x"][:, span(g * 2 * G, 2 * G), :]).then_inc(x_in[s], 16)

                for t in range(2):
                    step(Step(0, t, 4, EG))
                sp.wait_ge(zero_made, 1)
                flat = d["agg0"].rearrange("p t c -> p (t c)")
                with sp.Fori(0, ZN) as i:
                    sp.dma_start(flat[:, bass.ds(i * ZW, ZW)], zero[:, :]).then_inc(agg0_zeroed, 16)
                sp.dma_start(flat[:, ZN * ZW:TILES * C1], zero[:, 0:TILES * C1 - ZN * ZW]).then_inc(agg0_zeroed, 16)
                for t in range(2, 4):
                    step(Step(0, t, 4, EG))
                with sp.Fori(1, EG // 4) as it:
                    for pos in range(4):
                        step(Step(it, pos, 4))
                for t in range(EG // 4 * 4, EG):
                    step(Step(t // 4, t % 4, 4, EG))

            @block.gpsimd
            def _(pool):
                ph.prime(pool)
                pool.memset(zero[:, :], 0.0).then_inc(zero_made, 1)
                pool.memset(k.ident[:, :], 0.0).then_inc(masks_filled, 1)
                pool.memset(first[:, :, :], 1.0).then_inc(masks_filled, 1)
                pool.memset(msg[:, :, :, C:C1], 1.0).then_inc(ones_made, 1)
                pool.wait_ge(masks_filled, 2)
                pool.affine_select(out=k.ident[:, :], in_=k.ident[:, :], compare_op=ALU.not_equal, fill=1.0,
                                   base=0, pattern=[[-1, P]], channel_multiplier=1).then_inc(masks_made, 1)
                for u in range(2):
                    pool.affine_select(out=first[:, u, :], in_=first[:, u, :], compare_op=ALU.is_gt, fill=0.0,
                                       base=u * P, pattern=[[-1, 2 * P]], channel_multiplier=1).then_inc(masks_made, 1)
                for u in range(2):
                    pool.iota(dumpi[:, u:G:2], pattern=[[0, G // 2]], base=DUMP + u, channel_multiplier=TILES).then_inc(masks_made, 1)

                def gather(t, j):
                    s = t.slot(0, 4)
                    if j == 0:
                        pool.wait_ge(gidx_made, done(t.group(0)))
                        pool.wait_ge(h_made, ago(t.group(0), 4))
                        settle_waits(pool, pool_mark)
                    pool.indirect_dma_start(out=xs[:, s, j, :], out_offset=None, in_=xrows,
                                            in_offset=bass.IndirectOffsetOnAxis(ap=gidx[:, s, j:j + 1], axis=0)).then_inc(xs_in[s], 16)

                def scatter(t, j):
                    g = t.group(4)
                    if j == 0:
                        pool.wait_ge(tot_out, done(g))
                        pool.wait_ge(sidx_made, done(g))
                        if not t.again(4, 1):
                            pool.wait_ge(agg0_zeroed, 16 * (ZN + 1))
                    if j == 2 or j == 0 and t.again(4, 1):
                        for u in range(2):
                            pool.wait_ge(scattered[u], pairs_landed(g, j // 2))
                        settle_waits(pool, pool_mark)
                    pool.indirect_dma_start(out=aggrows, out_offset=bass.IndirectOffsetOnAxis(ap=sidx[:, t.slot(4), j:j + 1], axis=0),
                                            in_=tot[:, t.slot(4), j, :], in_offset=None, compute_op=ALU.add,
                                            bounds_check=P * TILES - 1, oob_is_err=True).then_inc(scattered[j % 2], 16)

                def step(t):
                    for half in range(2):
                        if t.live(4):
                            for j in (2 * half, 2 * half + 1):
                                scatter(t, j)
                        if t.live(0):
                            for j in (2 * half, 2 * half + 1):
                                gather(t, j)

                steps(pool, step)
                for u in range(2):
                    pool.wait_ge(scattered[u], pairs_landed(EG))

            @block.vector
            def _(dve):
                V = nc.vector
                V.memset(eaT[C:C1, :, :], 1.0).then_inc(ones_made, 1)
                dve.wait_ge(idx_in, 32)
                n = 0
                for of, to in ((srci, k.src_row), (dsti, k.dst_row)):
                    V.tensor_scalar(lo[:, :], of[:, :], P - 1, None, ALU.bitwise_and).then_inc(rows_made, 1)
                    V.tensor_scalar(hi[:, :], of[:, :], 7, None, ALU.logical_shift_right).then_inc(rows_made, 1)
                    dve.wait_ge(rows_made, n + 2)
                    V.scalar_tensor_tensor(to[:, :], lo[:, :], float(TILES), hi[:, :], ALU.mult, ALU.add).then_inc(rows_made, 1)
                    n += 3
                    dve.wait_ge(rows_made, n)
                V.tensor_copy(k.dst_f[:, :], dsti[:, :])
                dve.wait_ge(masks_made, 5)
                V.tensor_copy(dumpf[:, :], dumpi[:, :]).then_inc(rows_made, 1)
                dve.wait_ge(rows_made, n + 1)
                V.tensor_tensor(dump[:, :].rearrange("p (g j) -> p g j", j=G),
                                dumpf[:, :].rearrange("p (o j) -> p o j", o=1).broadcast_to([P, EG, G]),
                                k.dst_row[:, :].rearrange("p (g j) -> p g j", j=G), ALU.subtract).then_inc(rows_made, 1)
                dve.wait_ge(const_in, 16 * 12)
                V.tensor_scalar(k.one_eps[:, :], k.one_eps[:, :], 1.0, None, ALU.add)
                V.memset(k.ln_eps[:, :], LN_EPS).then_inc(rows_made, 1)
                dve.wait_ge(rows_made, n + 3)

                def step(t):
                    if t.live(0):
                        V.tensor_copy(gidx[:, t.slot(0, 4), :], k.src_row[:, tiles(t.group(0))]).then_inc(gidx_made, 1)
                    if t.live(3):
                        g, s = t.group(3), t.slot(3)
                        dve.wait_ge(srow_made, done(g))
                        if t.again(3):
                            for u in range(2):
                                dve.wait_ge(scattered[u], pairs_landed(g - 1))
                        settle_waits(dve, dve_mark)
                        V.tensor_copy(sidx[:, s, :], k.scatter_row[:, tiles(g)]).then_inc(sidx_made, 1)
                    if not t.live(2):
                        return
                    g, s = t.group(2), t.slot(2)
                    dve.wait_ge(x_in[s], landed(t.turn(2)))
                    dve.wait_ge(xs_in[t.slot(2, 4)], 16 * G * (t.turn(2, 4) + 1))
                    for j in range(G):
                        V.bn_stats(bn[:, s, j, :, :], xs[:, t.slot(2, 4), j, :])
                    for j in range(2 * G):
                        last = V.bn_stats(bn[:, s, G + j, :, :], k.R[:, span(g * 2 * G + j, 1), :])
                    last.then_inc(bn_made, 1)
                    dve.wait_ge(dr_in[s], landed(t.turn(2)))
                    dve.wait_ge(tot_made, ago(g, 2))
                    for j in range(G):
                        pair = dr[:, s, (j // 2) * 2 * P:(j // 2 + 1) * 2 * P]
                        last = V.tensor_scalar(S[:, s, j, :], pair, k.dst_f[:, span(g * G + j, 1)], None, ALU.is_equal)
                    last.then_inc(S_made, 1)
                    dve.wait_ge(bn_made, done(g))
                    V.tensor_tensor(mean2[:, s, :], bn[:, s, :, 0, 1], bn[:, s, :, 1, 1], ALU.add)
                    V.tensor_tensor(dif[:, s, :], bn[:, s, :, 0, 1], bn[:, s, :, 1, 1], ALU.subtract)
                    V.tensor_tensor(sq[:, s, :], bn[:, s, :, 0, 2], bn[:, s, :, 1, 2], ALU.add).then_inc(halves_made, 1)
                    dve.wait_ge(halves_made, done(g))
                    V.tensor_tensor(dif2[:, s, :], dif[:, s, :], dif[:, s, :], ALU.mult).then_inc(dif2_made, 1)
                    dve.wait_ge(dif2_made, done(g))
                    V.scalar_tensor_tensor(var4[:, s, :], sq[:, s, :], 4.0 / C, dif2[:, s, :], ALU.mult, ALU.add).then_inc(var_made, 1)
                    for j in range(G):
                        n = (j % 2 + 1) * P
                        at = (j // 2) * 2 * P
                        last = V.scalar_tensor_tensor(junk[:, j, 0:n], dr[:, s, at:at + n], k.dst_f[:, span(g * G + j, 1)],
                                                      first[:, j % 2, 0:n], ALU.is_equal, ALU.mult, accum_out=earlier[:, s, j:j + 1])
                    last.then_inc(earlier_made, 1)
                    dve.wait_ge(std_made, done(g))
                    V.reciprocal(rs[:, s, :], sd[:, s, :]).then_inc(rs_made, 1)
                    dve.wait_ge(rs_made, done(g))
                    V.scalar_tensor_tensor(nb[:, s, :], mean2[:, s, 0:G], -0.5, rs[:, s, 0:G], ALU.mult, ALU.mult).then_inc(nb_made, 1)
                    V.tensor_scalar(k.mean[:, span(g * 2 * G, 2 * G)], mean2[:, s, G:3 * G], 0.5, None, ALU.mult)
                    V.tensor_scalar(k.rstd[:, span(g * 2 * G, 2 * G)], rs[:, s, G:3 * G], k.one_eps[:, :], None, ALU.mult)
                    dve.wait_ge(earlier_made, done(g))
                    V.tensor_scalar(dup[:, s, :], earlier[:, s, :], 0.0, None, ALU.is_gt).then_inc(dup_made, 1)
                    dve.wait_ge(efr_made, done(g))
                    V.bn_stats(k.ef_bn[:, span(g, 1), :], efT[:, s, 0:EW_LAST if t.last(2) else W]).then_inc(efst_made, 1)
                    dve.wait_ge(dup_made, done(g))
                    V.tensor_tensor(shift[:, s, :], dup[:, s, :], dump[:, tiles(g)], ALU.mult).then_inc(shift_made, 1)
                    dve.wait_ge(shift_made, done(g))
                    V.tensor_tensor(k.scatter_row[:, tiles(g)], shift[:, s, :], k.dst_row[:, tiles(g)], ALU.add).then_inc(srow_made, 1)

                steps(dve, step)

            @block.scalar
            def _(act):
                A = nc.scalar
                act.wait_ge(rows_made, 9)

                def step(t):
                    if t.live(2):
                        g, s = t.group(2), t.slot(2)
                        act.wait_ge(ef_made, done(g))
                        act.wait_ge(efst_made, ago(g, 2))
                        A.activation(efT[:, s, :], ps_ef[s][:, :], ACT.Relu, bias=k.b_ef[:, :]).then_inc(efr_made, 1)
                        act.wait_ge(var_made, done(g))
                        act.wait_ge(rs_made, ago(g, 2))
                        A.activation(sd[:, s, :], var4[:, s, :], ACT.Sqrt, bias=k.ln_eps[:, :], scale=0.25).then_inc(std_made, 1)
                    if t.live(3):
                        g, s = t.group(3), t.slot(3)
                        act.wait_ge(tot_made, done(g))
                        if t.again(3):
                            for u in range(2):
                                act.wait_ge(scattered[u], pairs_landed(g - 1))
                        A.copy(tot[:, s, :, :], ps_tot[s][:, :, :]).then_inc(tot_out, 1)
                    if t.live(2):
                        g, s = t.group(2), t.slot(2)
                        act.wait_ge(nb_made, done(g))
                        act.wait_ge(pre_made, ago(g, 2))
                        for j in range(G):
                            last = A.activation(h[:, s, j, :], xs[:, t.slot(2, 4), j, :], ACT.Relu, bias=nb[:, s, j:j + 1], scale=rs[:, s, j:j + 1])
                        last.then_inc(h_made, 1)
                        act.wait_ge(pre_made, done(g))
                        act.wait_ge(tot_made, ago(g, 2))
                        A.activation(msg[:, s, :, 0:C], ps_pre[s][:, :, :], ACT.Relu).then_inc(msg_made, 1)

                steps(act, step)

            @block.tensor
            def _(pe):
                T = nc.tensor
                pe.wait_ge(const_in, 16 * 12)
                pe.wait_ge(masks_made, 5)
                pe.wait_ge(ones_made, 2)

                def step(t):
                    if t.live(2):
                        g, s = t.group(2), t.slot(2)
                        pe.wait_ge(ea4_in[s], landed(t.turn(2)))
                        pe.wait_ge(efr_made, ago(g, 2))
                        T.matmul(ps_ef[s][:, :], k.w_ef[:, :], ea4T[:, s, :], start=True, stop=True).then_inc(ef_made, 1)
                        pe.wait_ge(ea_in[s], landed(t.turn(2)))
                        pe.wait_ge(msg_made, ago(g, 2))
                    if t.live(3):
                        z = t.slot(3)
                        pe.wait_ge(S_made, done(t.group(3)))
                        pe.wait_ge(msg_made, done(t.group(3)))
                        pe.wait_ge(tot_out, ago(t.group(3), 2))
                        for j in range(G):
                            for u in range(2):
                                i = j // 2 * 2 + u
                                last = T.matmul(ps_tot[z][:, j, :], S[:, z, i, (j % 2) * P:(j % 2 + 1) * P], msg[:, z, i, :],
                                                start=(u == 0), stop=(u == 1))
                        last.then_inc(tot_made, 1)
                    if t.live(2):
                        for j in range(G):
                            last = T.matmul(ps_pre[s][:, j, :], eaT[:, s, j * P:(j + 1) * P], k.w_e0[:, :], start=True, stop=False)
                            if j == 0:
                                pe.wait_ge(h_made, done(g))
                            last = T.matmul(ps_pre[s][:, j, :], k.ident[:, :], h[:, s, j, :], start=False, stop=True)
                        last.then_inc(pre_made, 1)

                steps(pe, step)


def node_phase(nc, d, k):
    with Phase(nc, "n0") as ph:
        h0 = ph.sb("h0", [P, 2, G, C])
        agg = ph.sb("agg", [P, 4, G, C1])
        hhT = ph.sb("hhT", [UROWS, 2, W])
        r1T = ph.sb("r1T", [C1, 2, W])
        bn = ph.sb("bn", [P, 2, G, 6])
        mv = ph.sb("mean_var", [P, 2, G, 2])
        nm = ph.sb("less_mean", [P, 2, G])
        sd = ph.sb("std", [P, 2, G])
        rs = ph.sb("rstd", [P, 2, G])
        h1 = ph.sb("h1", [P, 4, G, C])
        zero = ph.sb("zero", [P, 2 * G, C])
        efmv = ph.sb("ef_mean_var", [C, 2])
        efsd = ph.sb("ef_std", [C, 1])
        efa = ph.sb("ef_scale", [C, 1])
        fold = ph.sb("ef_fold", [C, C1])
        ps_T = [ph.ps(f"T{s}", [C1, W]) for s in range(2)]
        ps_1 = [ph.ps(f"w1{s}", [C, W]) for s in range(2)]
        ps_2 = [ph.ps(f"w2{s}", [P, G, C]) for s in range(2)]
        ps_f = ph.ps("fold", [C1, C])

        setup = ph.sem("setup")
        std_ef, fold_made, zero_made, ones_made = (ph.sem(n) for n in ("std_ef", "fold_made", "zero_made", "ones_made"))
        agg_in, h1_out, rows_out = ph.sems("agg_in", 4), ph.sems("h1_out", 4), ph.sems("rows_out")
        agg1_zeroed = ph.sem("agg1_zeroed")
        less_made, h0_made, hh_made = ph.count("less_made"), ph.count("h0_made"), ph.count("hh_made")
        T_made, hhT_made, w1_made, r1_made = (ph.count(n) for n in ("T_made", "hhT_made", "w1_made", "r1_made"))
        w2_made, x1_made, bn_made, mv_made = (ph.count(n) for n in ("w2_made", "x1_made", "bn_made", "mv_made"))
        nm_made, std_made, relu_made, rs_made, h1_made = (ph.count(n) for n in ("nm_made", "std_made", "relu_made", "rs_made", "h1_made"))
        pool_mark, dve_mark, act_mark = ph.sem("pool_mark"), ph.sem("dve_mark"), ph.sem("act_mark")
        LAG = 11

        def steps(eng, step):
            run_steps(eng, NG, LAG, step, 4)

        with nc.Block() as block:

            @block.sync
            def _(sp):
                sp.wait_ge(zero_made, 1)
                sp.dma_start(d["agg1"][:, NT:TILES, :], zero[:, 0:TILES - NT, :]).then_inc(agg1_zeroed, 16)
                sp.dma_start(d["h1"][:, NT:TILES, :], zero[:, 0:TILES - NT, :]).then_inc(agg1_zeroed, 16)

                def step(t):
                    if t.live(11):
                        g, s = t.group(11), t.slot(11, 4)
                        sp.wait_ge(h1_made, done(g))
                        sp.dma_start(d["h1"][:, tiles(g), :], h1[:, s, :, :]).then_inc(h1_out[s], 16)
                    if t.live(0):
                        g, s = t.group(0), t.slot(0, 4)
                        sp.wait_ge(T_made, ago(g, 4))
                        sp.dma_start(agg[:, s, :, :], d["agg0"][:, tiles(g), :]).then_inc(agg_in[s], 16)
                        if t.pos % 2 == 0:
                            sp.dma_start(d["agg1"][:, tiles(g, 2 * G), :], zero[:, :, :]).then_inc(agg1_zeroed, 16)
                    if t.live(5):
                        g, s = t.group(5), t.slot(5)
                        sp.wait_ge(hhT_made, done(g))
                        sp.dma_start(d["uT"][DEGREE:UROWS, span(g * W, W)], hhT[DEGREE:UROWS, s, :]).then_inc(rows_out[s], 16)

                steps(sp, step)
                sp.wait_ge(agg1_zeroed, 16 * (NG // 2 + 2))
                for s in range(4):
                    sp.wait_ge(h1_out[s], landed(-(-(NG - s) // 4)))
                for s in range(2):
                    sp.wait_ge(rows_out[s], landed(NG // 2))

            @block.gpsimd
            def _(pool):
                ph.prime(pool)
                for out in h1_out + rows_out:
                    pool.sem_inc(out, 16)
                pool.memset(zero[:, :, :], 0.0).then_inc(zero_made, 1)

                def step(t):
                    if t.live(2):
                        g, s = t.group(2), t.slot(2, 4)
                        pool.wait_ge(h0_made, done(g))
                        pool.wait_ge(agg_in[s], landed(t.turn(2, 4)))
                        pool.tensor_tensor(agg[:, s, :, 0:C], h0[:, t.slot(2), :, :], agg[:, s, :, 0:C], ALU.add).then_inc(hh_made, 1)
                    if t.live(0):
                        g, s = t.group(0), t.slot(0)
                        pool.wait_ge(hh_made, ago(g, 2))
                        pool.tensor_tensor(h0[:, s, :, :], k.R[:, tiles(g), :], per_tile(k.mean[:, tiles(g)]), ALU.subtract).then_inc(less_made, 1)

                steps(pool, step)

            @block.scalar
            def _(act):
                A = nc.scalar
                act.wait_ge(setup, 1)
                A.activation(efsd[:, :], efmv[:, 1:2], ACT.Sqrt, bias=k.ln_eps[0:C, :]).then_inc(std_ef, 1)
                act.wait_ge(ones_made, 2)

                def step(t):
                    if t.live(9):
                        g, s = t.group(9), t.slot(9)
                        act.wait_ge(nm_made, done(g))
                        act.wait_ge(rs_made, ago(g, 2))
                        A.activation(sd[:, s, :], mv[:, s, :, 1], ACT.Sqrt, bias=k.ln_eps[:, :]).then_inc(std_made, 1)
                        act.wait_ge(h1_out[t.slot(9, 4)], landed(t.turn(9, 4)))
                        for j in range(G):
                            last = A.activation(h1[:, t.slot(9, 4), j, :], k.R[:, span(g * G + j, 1), :], ACT.Relu, bias=nm[:, s, j:j + 1])
                        last.then_inc(relu_made, 1)
                    if t.live(4):
                        g, s = t.group(4), t.slot(4)
                        act.wait_ge(T_made, done(g))
                        act.wait_ge(w1_made, ago(g, 2))
                        act.wait_ge(rows_out[s], landed(t.turn(4)))
                        A.copy(hhT[0:C1, s, :], ps_T[s][:, :]).then_inc(hhT_made, 1)
                    if t.live(6):
                        g, s = t.group(6), t.slot(6)
                        act.wait_ge(w1_made, done(g))
                        act.wait_ge(w2_made, ago(g, 2))
                        A.activation(r1T[0:C, s, :], ps_1[s][:, :], ACT.Relu, bias=k.b1[:, :]).then_inc(r1_made, 1)

                steps(act, step)

            @block.vector
            def _(dve):
                V = nc.vector
                V.memset(r1T[C:C1, :, :], 1.0).then_inc(ones_made, 1)
                V.memset(hhT[C:UROWS, :, :], 1.0).then_inc(ones_made, 1)
                V.bn_aggr(efmv[:, :], k.ef_bn[:, :, :]).then_inc(setup, 1)
                dve.wait_ge(std_ef, 1)
                V.reciprocal(efa[:, :], efsd[:, :]).then_inc(setup, 1)
                dve.wait_ge(setup, 2)
                V.tensor_tensor(efa[:, :], efa[:, :], k.bn_gb[:, 2:3], ALU.mult).then_inc(setup, 1)
                dve.wait_ge(setup, 3)
                V.tensor_scalar(fold[:, 0:C], k.ident[0:C, 0:C], efa[:, :], None, ALU.mult)
                V.tensor_tensor(fold[:, C:C1], efmv[:, 0:1], efa[:, :], ALU.mult).then_inc(setup, 1)
                dve.wait_ge(setup, 4)
                V.tensor_tensor(fold[:, C:C1], k.bn_gb[:, 3:4], fold[:, C:C1], ALU.subtract).then_inc(setup, 1)
                dve.wait_ge(fold_made, 1)
                V.tensor_copy(k.w_ef_msg[0:C, :], ps_f[0:C, :])
                V.tensor_tensor(k.w_ef_msg[C:C1, :], ps_f[C:C1, :], k.b_msg[C:C1, :], ALU.add)

                def step(t):
                    if t.live(8):
                        g, s = t.group(8), t.slot(8)
                        dve.wait_ge(w2_made, done(g))
                        V.tensor_tensor(k.R[:, tiles(g), :], ps_2[s][:, :, :], k.R[:, tiles(g), :], ALU.add).then_inc(x1_made, 1)
                    if t.live(1):
                        g, s = t.group(1), t.slot(1)
                        dve.wait_ge(less_made, done(g))
                        V.scalar_tensor_tensor(h0[:, s, :, :], h0[:, s, :, :], 0.0, per_tile(k.rstd[:, tiles(g)]), ALU.max, ALU.mult).then_inc(h0_made, 1)
                    if t.live(8):
                        g, s = t.group(8), t.slot(8)
                        dve.wait_ge(x1_made, done(g))
                        settle_waits(dve, dve_mark)
                        for j in range(G):
                            last = V.bn_stats(bn[:, s, j, :], k.R[:, span(g * G + j, 1), :])
                        last.then_inc(bn_made, 1)
                    if t.live(10):
                        g, s = t.group(10), t.slot(10)
                        dve.wait_ge(std_made, done(g))
                        V.reciprocal(rs[:, s, :], sd[:, s, :]).then_inc(rs_made, 1)
                    if t.live(8):
                        g, s = t.group(8), t.slot(8)
                        dve.wait_ge(bn_made, done(g))
                        dve.wait_ge(relu_made, ago(g, 2))
                        settle_waits(dve, dve_mark)
                        for j in range(G):
                            last = V.bn_aggr(mv[:, s, j, :], bn[:, s, j, :])
                        last.then_inc(mv_made, 1)
                    if t.live(10):
                        g, s = t.group(10), t.slot(10)
                        dve.wait_ge(relu_made, done(g))
                        dve.wait_ge(rs_made, done(g))
                        V.tensor_tensor(h1[:, t.slot(10, 4), :, :], h1[:, t.slot(10, 4), :, :], per_tile(rs[:, s, :]), ALU.mult).then_inc(h1_made, 1)
                    if t.live(8):
                        g, s = t.group(8), t.slot(8)
                        dve.wait_ge(mv_made, done(g))
                        V.tensor_scalar(nm[:, s, :], mv[:, s, :, 0], -1.0, None, ALU.mult).then_inc(nm_made, 1)

                steps(dve, step)

            @block.tensor
            def _(pe):
                T = nc.tensor
                pe.wait_ge(setup, 5)
                T.matmul(ps_f[:, :], fold[:, :], k.w_msg[:, 2, :], start=True, stop=True).then_inc(fold_made, 1)
                pe.wait_ge(ones_made, 2)

                def step(t):
                    if t.live(7):
                        g, s = t.group(7), t.slot(7)
                        pe.wait_ge(r1_made, done(g))
                        pe.wait_ge(x1_made, ago(g, 2))
                        for j in range(G):
                            last = T.matmul(ps_2[s][:, j, :], r1T[:, s, j * P:(j + 1) * P], k.w2[:, :], start=True, stop=True)
                        last.then_inc(w2_made, 1)
                    if t.live(3):
                        g, s = t.group(3), t.slot(3)
                        pe.wait_ge(hh_made, done(g))
                        pe.wait_ge(hhT_made, ago(g, 2))
                        for j in range(G):
                            last = T.transpose(ps_T[s][:, j * P:(j + 1) * P], agg[:, t.slot(3, 4), j, :], k.ident[:, :])
                        last.then_inc(T_made, 1)
                    if t.live(5):
                        g, s = t.group(5), t.slot(5)
                        pe.wait_ge(hhT_made, done(g))
                        pe.wait_ge(r1_made, ago(g, 2))
                        T.matmul(ps_1[s][:, :], k.w1[:, :], hhT[0:C, s, :], start=True, stop=True).then_inc(w1_made, 1)

                steps(pe, step)


def edge_phase_1(nc, d, k):
    with Phase(nc, "e1") as ph:
        hs = ph.sb("h_src", [P, 4, G, C])
        hd = ph.sb("h_dst", [P, 4, G, C])
        ea4T = ph.sb("ea4T", [CE, 2, W])
        dr = ph.sb("dst_row", [P, 2, W], INT32)
        hsT = ph.sb("h_srcT", [C, W])
        hdT = ph.sb("h_dstT", [C, W])
        efT = ph.sb("efT", [C1, W])
        msg = ph.sb("msg", [P, 2, G, C1])
        S = ph.sb("same_dst", [P, 2, G, 2 * P])
        tot = ph.sb("tot", [P, 2, G, C])
        gidx = ph.sb("gather_idx", [P, 4, 2, G], INT32)
        sidx = ph.sb("scatter_idx", [P, 2, G], INT32)
        h1 = ph.sb("h1", [P, 2, G, C])
        h1T = ph.sb("h1T", [C, 2, W])
        uT = ph.sb("uT", [C, 2, W])
        nothing = ph.sb("nothing", [P, C1])
        ps_s = ph.ps("sT", [C, W])
        ps_d = ph.ps("dT", [C, W])
        ps_ef = ph.ps("ef", [C, W])
        ps_m = ph.ps("m", [P, G, C])
        ps_tot = ph.ps("tot", [P, G, C])
        ps_hT = ph.ps("hT", [C, W])
        ps_u = ph.ps("u", [C, W])
        ps_gram = ph.ps("gram", [C, C1])

        ones_made, nothing_made = ph.sem("ones_made"), ph.sem("nothing_made")
        ea4_in, dr_in, scattered = (ph.sems(n) for n in ("ea4_in", "dr_in", "scattered"))
        hs_in, hd_in = ph.sems("hs_in", 4), ph.sems("hd_in", 4)
        h1_in, uT_out = ph.sems("h1_in"), ph.sems("uT_out")
        gidx_made, sidx_made, S_made, sT_out, dT_out = (ph.count(n) for n in ("gidx_made", "sidx_made", "S_made", "sT_out", "dT_out"))
        s_made, d_made, ef_made, ef_out = (ph.count(n) for n in ("s_made", "d_made", "ef_made", "ef_out"))
        m_made, msg_made, tot_made, tot_out = (ph.count(n) for n in ("m_made", "msg_made", "tot_made", "tot_out"))
        hT_made, hT_out, u_made, uT_made, ubn_made = (ph.count(n) for n in ("hT_made", "hT_out", "u_made", "uT_made", "ubn_made"))
        gram_made = ph.sem("gram_made")
        pool_mark, dve_mark = ph.sem("pool_mark"), ph.sem("dve_mark")

        hrows = d["h1"].rearrange("p t c -> (p t) c")
        aggrows = d["agg1"].rearrange("p t c -> (p t) c")
        LAG = 4

        def steps(eng, step):
            run_steps(eng, EG, LAG, step, 4)

        with nc.Block() as block:

            @block.sync
            def _(sp):
                def step(t):
                    if t.live(2):
                        for v in range(2):
                            u = t.group(2) * 2 + v
                            sp.wait_ge(uT_made, done(u))
                            sp.dma_start(d["uT"][0:C, span(u * W, W)], uT[:, v, :]).then_inc(uT_out[v], 16)
                    if t.live(0):
                        g, s = t.group(0), t.slot(0)
                        for v in range(2):
                            u = g * 2 + v
                            sp.wait_ge(hT_made, ago(u, 2))
                            sp.dma_start(h1[:, v, :, :], d["h1"][:, tiles(u), :]).then_inc(h1_in[v], 16)
                        sp.wait_ge(ef_made, ago(g, 2))
                        sp.dma_start(ea4T[:, s, :], d["ea4T"][:, span(g * W, W)]).then_inc(ea4_in[s], 16)
                        sp.wait_ge(S_made, ago(g, 2))
                        sp.dma_start(dr[:, s, :], d["dst_row"][:, span(g * W, W)].broadcast_to([P, W])).then_inc(dr_in[s], 16)

                steps(sp, step)
                for v in range(2):
                    sp.wait_ge(uT_out[v], landed(EG))

            @block.gpsimd
            def _(pool):
                ph.prime(pool)
                pool.memset(msg[:, :, :, C:C1], 1.0).then_inc(ones_made, 1)
                pool.memset(nothing[:, :], 0.0).then_inc(nothing_made, 1)
                for v in range(2):
                    pool.sem_inc(uT_out[v], 16)

                def gather(t, j):
                    g, s = t.group(0), t.slot(0, 4)
                    if j == 0:
                        pool.wait_ge(gidx_made, done(g))
                        pool.wait_ge(s_made, ago(g, 4))
                        pool.wait_ge(d_made, ago(g, 4))
                        settle_waits(pool, pool_mark)
                    for v, (to, got) in enumerate(((hs, hs_in), (hd, hd_in))):
                        pool.indirect_dma_start(out=to[:, s, j, :], out_offset=None, in_=hrows,
                                                in_offset=bass.IndirectOffsetOnAxis(ap=gidx[:, s, v, j:j + 1], axis=0)).then_inc(got[s], 16)

                def scatter(t, j):
                    g = t.group(4)
                    if j == 0:
                        pool.wait_ge(tot_out, done(g))
                        pool.wait_ge(sidx_made, done(g))
                    if j == 2 or j == 0 and t.again(4, 1):
                        for u in range(2):
                            pool.wait_ge(scattered[u], pairs_landed(g, j // 2))
                        settle_waits(pool, pool_mark)
                    pool.indirect_dma_start(out=aggrows, out_offset=bass.IndirectOffsetOnAxis(ap=sidx[:, t.slot(4), j:j + 1], axis=0),
                                            in_=tot[:, t.slot(4), j, :], in_offset=None, compute_op=ALU.add,
                                            bounds_check=P * TILES - 1, oob_is_err=True).then_inc(scattered[j % 2], 16)

                def step(t):
                    for half in range(2):
                        if t.live(0):
                            for j in (2 * half, 2 * half + 1):
                                gather(t, j)
                        if t.live(4):
                            for j in (2 * half, 2 * half + 1):
                                scatter(t, j)

                steps(pool, step)
                for u in range(2):
                    pool.wait_ge(scattered[u], pairs_landed(EG))

            @block.vector
            def _(dve):
                V = nc.vector
                V.memset(efT[C:C1, :], 1.0).then_inc(ones_made, 1)

                def indices(t):
                    g, s = t.group(0), t.slot(0, 4)
                    if t.again(0, 4):
                        dve.wait_ge(hs_in[s], 16 * G * t.turn(0, 4))
                        dve.wait_ge(hd_in[s], 16 * G * t.turn(0, 4))
                        settle_waits(dve, dve_mark)
                    V.tensor_copy(gidx[:, s, 0, :], k.src_row[:, tiles(g)])
                    V.tensor_copy(gidx[:, s, 1, :], k.dst_row[:, tiles(g)]).then_inc(gidx_made, 1)

                def step(t):
                    if t.live(0):
                        indices(t)
                    if t.live(2):
                        g, s = t.group(2), t.slot(2)
                        dve.wait_ge(d_made, done(g))
                        dve.wait_ge(m_made, ago(g, 1))
                        V.tensor_copy(hdT[:, :], ps_d[:, :]).then_inc(dT_out, 1)
                    if t.live(1):
                        for v in range(2):
                            u = t.group(1) * 2 + v
                            dve.wait_ge(hT_made, done(u))
                            dve.wait_ge(u_made, ago(u, 2))
                            V.tensor_copy(h1T[:, v, :], ps_hT[:, :]).then_inc(hT_out, 1)
                    if t.live(2):
                        dve.wait_ge(dr_in[s], landed(t.turn(2)))
                        dve.wait_ge(tot_made, ago(g, 2))
                        for j in range(G):
                            pair = dr[:, s, (j // 2) * 2 * P:(j // 2 + 1) * 2 * P]
                            last = V.tensor_scalar(S[:, s, j, :], pair, k.dst_f[:, span(g * G + j, 1)], None, ALU.is_equal)
                        last.then_inc(S_made, 1)
                    if t.live(3):
                        g, s = t.group(3), t.slot(3)
                        if t.again(3):
                            for u in range(2):
                                dve.wait_ge(scattered[u], pairs_landed(g - 1))
                        settle_waits(dve, dve_mark)
                        V.tensor_copy(sidx[:, s, :], k.scatter_row[:, tiles(g)]).then_inc(sidx_made, 1)
                    if t.live(1):
                        for v in range(2):
                            u = t.group(1) * 2 + v
                            dve.wait_ge(uT_made, done(u))
                            settle_waits(dve, dve_mark)
                            V.bn_stats(k.u_bn[:, span(u, 1), :], uT[:, v, 0:NW_LAST if v and t.last(1) else W]).then_inc(ubn_made, 1)

                steps(dve, step)
                dve.wait_ge(gram_made, 1)
                V.tensor_copy(k.gram[:, :], ps_gram[:, :])

            @block.scalar
            def _(act):
                A = nc.scalar

                def step(t):
                    if t.live(3):
                        g, s = t.group(3), t.slot(3)
                        act.wait_ge(m_made, done(g))
                        act.wait_ge(tot_made, ago(g, 2))
                        A.activation(msg[:, s, :, 0:C], ps_m[:, :, :], ACT.Relu).then_inc(msg_made, 1)
                    if t.live(2):
                        g = t.group(2)
                        act.wait_ge(s_made, done(g))
                        act.wait_ge(m_made, ago(g, 1))
                        A.copy(hsT[:, :], ps_s[:, :]).then_inc(sT_out, 1)
                        act.wait_ge(ef_made, done(g))
                        A.activation(efT[0:C, :], ps_ef[:, :], ACT.Relu, bias=k.b_ef[:, :]).then_inc(ef_out, 1)
                    if t.live(3):
                        g, s = t.group(3), t.slot(3)
                        act.wait_ge(tot_made, done(g))
                        if t.again(3):
                            for w in range(2):
                                act.wait_ge(scattered[w], pairs_landed(g - 1))
                        A.copy(tot[:, s, :, :], ps_tot[:, :, :]).then_inc(tot_out, 1)
                    if t.live(1):
                        for v in range(2):
                            u = t.group(1) * 2 + v
                            act.wait_ge(u_made, done(u))
                            act.wait_ge(ubn_made, ago(u, 2))
                            act.wait_ge(uT_out[v], landed(t.group(1)))
                            A.activation(uT[:, v, :], ps_u[:, :], ACT.Relu, bias=k.b_node[:, :]).then_inc(uT_made, 1)

                steps(act, step)

            @block.tensor
            def _(pe):
                T = nc.tensor
                pe.wait_ge(nothing_made, 1)
                pe.wait_ge(ones_made, 2)
                T.matmul(ps_gram[:, :], nothing[:, 0:C], nothing[:, :], start=True, stop=False)

                def transposes(to, of, s, made):
                    for j in range(G):
                        last = T.transpose(to[:, j * P:(j + 1) * P], of[:, s, j, :], k.ident[:, :])
                    last.then_inc(made, 1)

                def node_T(t, v):
                    u = t.group(1) * 2 + v
                    pe.wait_ge(h1_in[v], landed(t.group(1)))
                    pe.wait_ge(hT_out, ago(u, 1))
                    transposes(ps_hT, h1, v, hT_made)

                def node_mm(t, v):
                    u = t.group(1) * 2 + v
                    pe.wait_ge(hT_out, done(u))
                    pe.wait_ge(uT_made, ago(u, 1))
                    T.matmul(ps_u[:, :], k.w_node[:, :], h1T[:, v, :], start=True, stop=True).then_inc(u_made, 1)

                def step(t):
                    if t.live(3):
                        g, s = t.group(3), t.slot(3)
                        pe.wait_ge(sT_out, done(g))
                        pe.wait_ge(dT_out, done(g))
                        pe.wait_ge(ef_out, done(g))
                        pe.wait_ge(msg_made, ago(g, 1))
                        for j in range(G):
                            for n, (x, w) in enumerate(((hsT, k.w_msg[:, 0, :]), (hdT, k.w_msg[:, 1, :]), (efT, k.w_ef_msg[:, :]))):
                                last = T.matmul(ps_m[:, j, :], x[:, j * P:(j + 1) * P], w, start=(n == 0), stop=(n == 2))
                        last.then_inc(m_made, 1)
                    if t.live(2):
                        g, s = t.group(2), t.slot(2, 4)
                        pe.wait_ge(hs_in[s], 16 * G * (t.turn(2, 4) + 1))
                        pe.wait_ge(sT_out, ago(g, 1))
                        transposes(ps_s, hs, s, s_made)
                        pe.wait_ge(hd_in[s], 16 * G * (t.turn(2, 4) + 1))
                        pe.wait_ge(dT_out, ago(g, 1))
                        transposes(ps_d, hd, s, d_made)
                        pe.wait_ge(ea4_in[t.slot(2)], landed(t.turn(2)))
                        pe.wait_ge(ef_out, ago(g, 1))
                        T.matmul(ps_ef[:, :], k.w_ef[:, :], ea4T[:, t.slot(2), :], start=True, stop=True).then_inc(ef_made, 1)
                    if t.live(1):
                        node_T(t, 0)
                    if t.live(3):
                        g, s = t.group(3), t.slot(3)
                        pe.wait_ge(msg_made, done(g))
                        for j in range(G):
                            r = EDGES_LAST if j == G - 1 and t.last(3) else P
                            last = T.matmul(ps_gram[:, :], msg[0:r, s, j, 0:C], msg[0:r, s, j, :], start=False, stop=(r < P))
                        if t.last(3):
                            last.then_inc(gram_made, 1)
                        pe.wait_ge(S_made, done(g))
                        pe.wait_ge(tot_out, ago(g, 1))
                        for j in range(G):
                            for u in range(2):
                                i = j // 2 * 2 + u
                                last = T.matmul(ps_tot[:, j, :], S[:, s, i, (j % 2) * P:(j % 2 + 1) * P], msg[:, s, i, 0:C],
                                                start=(u == 0), stop=(u == 1))
                        last.then_inc(tot_made, 1)
                    if t.live(1):
                        node_T(t, 1)
                        for v in range(2):
                            node_mm(t, v)

                steps(pe, step)


def final_phase(nc, d, k):
    with Phase(nc, "f") as ph:
        agg = ph.sb("agg", [P, 4, G, C])
        uT = ph.sb("uT", [UROWS, 4, W])
        y = ph.sb("y", [P, 4, G, C])
        st = ph.sb("stats", [C, 2, 2])
        tmp = ph.sb("tmp", [C, C])
        sd = ph.sb("std", [C, 2])
        scale = ph.sb("scale", [C, 2])
        shift = ph.sb("shift", [C, 2])
        fold = ph.sb("fold", [C, UROWS])
        a_col = ph.sb("scale_column", [C, P])
        a_row = ph.sb("scale_row", [P, C])
        w = ph.sb("w_out", [UROWS, C])
        ps_f = ph.ps("fold", [UROWS, C])
        ps_a = ph.ps("scale_row", [P, C])
        ps_y = [ph.ps(f"y{s}", [P, G, C]) for s in range(2)]

        setup, std_made, fold_made = (ph.sem(n) for n in ("setup", "std_made", "fold_made"))
        agg_in, uT_in, y_out = ph.sems("agg_in", 4), ph.sems("uT_in", 4), ph.sems("y_out", 4)
        scaled, ps_made, sum_made, y_made = (ph.count(n) for n in ("scaled", "ps_made", "sum_made", "y_made"))
        pool_mark, dve_mark = ph.sem("pool_mark"), ph.sem("dve_mark")
        SETUP = 9
        LAG = 5

        def steps(eng, step):
            run_steps(eng, NG, LAG, step, 4)

        with nc.Block() as block:

            @block.sync
            def _(sp):
                def step(t):
                    if t.live(0):
                        g, s = t.group(0), t.slot(0, 4)
                        sp.wait_ge(y_made, ago(g, 4))
                        sp.dma_start(agg[:, s, :, :], d["agg1"][:, tiles(g), :]).then_inc(agg_in[s], 16)
                        sp.wait_ge(ps_made, ago(g, 4))
                        sp.dma_start(uT[:, s, :], d["uT"][:, span(g * W, W)]).then_inc(uT_in[s], 16)

                steps(sp, step)

            @block.gpsimd
            def _(pool):
                ph.prime(pool)
                for out in y_out:
                    pool.sem_inc(out, 16)

                def step(t):
                    if t.live(4):
                        g, s = t.group(4), t.slot(4, 4)
                        pool.wait_ge(sum_made, done(g))
                        pool.wait_ge(scaled, done(g))
                        pool.tensor_tensor(y[:, s, :, :], y[:, s, :, :], agg[:, s, :, :], ALU.add).then_inc(y_made, 1)

                steps(pool, step)

            @block.vector
            def _(dve):
                V = nc.vector
                n = 0

                def settle(ins):
                    nonlocal n
                    n += 1
                    ins.then_inc(setup, 1)
                    dve.wait_ge(setup, n)

                V.bn_aggr(st[:, 0, :], k.u_bn[:, :, :])
                V.tensor_scalar(st[:, 1, 0:1], k.gram[:, C:C1], 1.0 / EDGES, None, ALU.mult)
                settle(V.tensor_tensor(tmp[:, :], k.gram[:, 0:C], k.ident[0:C, 0:C], ALU.mult))
                settle(V.reduce_sum(st[:, 1, 1:2], tmp[:, :], AX.X))
                settle(V.tensor_tensor(sd[:, 1:2], st[:, 1, 0:1], st[:, 1, 0:1], ALU.mult))
                settle(V.scalar_tensor_tensor(st[:, 1, 1:2], st[:, 1, 1:2], 1.0 / EDGES, sd[:, 1:2], ALU.mult, ALU.subtract))
                dve.wait_ge(std_made, 1)
                settle(V.reciprocal(scale[:, :], sd[:, :]))
                settle(V.tensor_tensor(scale[:, :], scale[:, :], k.bn_gb[:, 0:5:4], ALU.mult))
                settle(V.tensor_tensor(shift[:, :], st[:, :, 0], scale[:, :], ALU.mult))
                settle(V.tensor_tensor(shift[:, :], k.bn_gb[:, 1:6:4], shift[:, :], ALU.subtract))
                V.tensor_scalar(fold[:, 0:C], k.ident[0:C, 0:C], scale[:, 0:1], None, ALU.mult)
                V.tensor_copy(fold[:, DEGREE:DEGREE + 1], shift[:, 1:2])
                V.tensor_copy(fold[:, ONES:ONES + 1], shift[:, 0:1])
                settle(V.tensor_copy(a_col[:, :], scale[:, 1:2].broadcast_to([C, P])))
                assert n == SETUP
                dve.wait_ge(fold_made, 1)
                V.tensor_copy(w[:, :], ps_f[:, :])
                settle(V.tensor_copy(a_row[:, :], ps_a[:, :]))
                a_rows = a_row[:, :].rearrange("p (o c) -> p o c", o=1).broadcast_to([P, G, C])

                def step(t):
                    if t.live(3):
                        g, s = t.group(3), t.slot(3, 4)
                        dve.wait_ge(ps_made, done(g))
                        dve.wait_ge(y_out[s], landed(t.turn(3, 4)))
                        V.tensor_tensor(y[:, s, :, :], ps_y[t.slot(3)][:, :, :], k.R[:, tiles(g), :], ALU.add).then_inc(sum_made, 1)
                    if t.live(2):
                        g, s = t.group(2), t.slot(2, 4)
                        dve.wait_ge(agg_in[s], landed(t.turn(2, 4)))
                        V.tensor_tensor(agg[:, s, :, :], agg[:, s, :, :], a_rows, ALU.mult).then_inc(scaled, 1)

                steps(dve, step)

            @block.scalar
            def _(act):
                A = nc.scalar
                act.wait_ge(setup, 4)
                A.activation(sd[:, :], st[:, :, 1], ACT.Sqrt, bias=k.ln_eps[0:C, :]).then_inc(std_made, 1)

                def step(t):
                    if t.live(5):
                        g, s = t.group(5), t.slot(5, 4)
                        act.wait_ge(y_made, done(g))
                        act.dma_start(d["out"][:, tiles(g), :], y[:, s, :, :]).then_inc(y_out[s], 16)

                steps(act, step)
                for s in range(4):
                    act.wait_ge(y_out[s], landed(-(-(NG - s) // 4)))

            @block.tensor
            def _(pe):
                T = nc.tensor
                pe.wait_ge(setup, SETUP)
                T.matmul(ps_a[:, :], a_col[:, :], k.ident[0:C, 0:C], start=True, stop=True)
                T.matmul(ps_f[:, :], fold[:, :], k.ident[0:C, 0:C], start=True, stop=True).then_inc(fold_made, 1)
                pe.wait_ge(setup, SETUP + 1)

                def step(t):
                    if t.live(2):
                        g, s = t.group(2), t.slot(2, 4)
                        pe.wait_ge(uT_in[s], landed(t.turn(2, 4)))
                        pe.wait_ge(sum_made, ago(g, 2))
                        for j in range(G):
                            last = T.matmul(ps_y[t.slot(2)][:, j, :], uT[:, s, j * P:(j + 1) * P], w[:, :], start=True, stop=True)
                        last.then_inc(ps_made, 1)

                steps(pe, step)


def gnn_kernel(nc, d):
    with Phase(nc, "all") as ph:
        k = Kept()
        k.R = ph.sb("x", [P, NT, C])
        k.rstd = ph.sb("rstd", [P, NT])
        k.mean = ph.sb("mean", [P, NT])
        k.src_row = ph.sb("src_row", [P, ET], INT32)
        k.dst_row = ph.sb("dst_row", [P, ET], INT32)
        k.dst_f = ph.sb("dst_f", [P, ET])
        k.scatter_row = ph.sb("scatter_row", [P, ET], INT32)
        k.ident = ph.sb("ident", [P, P])
        k.ln_eps = ph.sb("ln_eps", [P, 1])
        k.one_eps = ph.sb("one_eps", [P, 1])
        k.w_e0 = ph.sb("w_e0", [C1, C])
        k.w_ef = ph.sb("w_ef", [CE, C])
        k.b_ef = ph.sb("b_ef", [C, 1])
        k.w1 = ph.sb("w1", [C, C])
        k.b1 = ph.sb("b1", [C, 1])
        k.w2 = ph.sb("w2", [C1, C])
        k.w_node = ph.sb("w_node", [C, C])
        k.b_node = ph.sb("b_node", [C, 1])
        k.w_msg = ph.sb("w_msg", [C, 3, C])
        k.b_msg = ph.sb("b_msg", [C1, C])
        k.w_ef_msg = ph.sb("w_ef_msg", [C1, C])
        k.bn_gb = ph.sb("bn_gb", [C, 6])
        k.ef_bn = ph.sb("ef_bn", [C, EG, 6])
        k.u_bn = ph.sb("u_bn", [C, NG, 6])
        k.gram = ph.sb("gram", [C, C1])
        edge_phase_0(nc, d, k)
        node_phase(nc, d, k)
        edge_phase_1(nc, d, k)
        final_phase(nc, d, k)


def kernel(x, src, dst, edge_attr_4, edge_attr_96, L0_gnn_W_edge, L0_gnn_b_edge, L0_gnn_eps, L0_gnn_W1, L0_gnn_b1,
           L0_gnn_W2, L0_gnn_b2, L1_gnn_W_node, L1_gnn_b_node, L1_gnn_g_node, L1_gnn_beta_node, L1_gnn_W_edge,
           L1_gnn_b_edge, L1_gnn_g_edge, L1_gnn_beta_edge, L1_gnn_W_msg, L1_gnn_b_msg, L1_gnn_g_msg, L1_gnn_beta_msg):
    import numpy as np
    from concourse import bacc
    from concourse.bass_utils import run_bass_kernel_spmd

    def table(a):
        padded = np.zeros((TILES * P, a.shape[1]), a.dtype)
        padded[:a.shape[0]] = a
        return np.ascontiguousarray(padded.reshape(TILES, P, -1).transpose(1, 0, 2))

    def edges(a, fill):
        padded = np.full(ET * P, fill, np.int32)
        padded[:EDGES] = a
        return padded

    def transposed(a):
        padded = np.zeros((a.shape[1], ET * P), a.dtype)
        padded[:, :EDGES] = np.asarray(a).T
        return padded

    def column(a):
        return np.asarray(a).reshape(-1, 1)

    x, src, dst = np.asarray(x), np.asarray(src), np.asarray(dst)
    src_p, dst_p = edges(src, 0), edges(dst, DUMP * P)
    arrays = {
        "x": table(x),
        "src_col": src_p.reshape(ET, P).T, "dst_col": dst_p.reshape(ET, P).T, "dst_row": dst_p.reshape(1, -1),
        "eaT": transposed(edge_attr_96), "ea4T": transposed(edge_attr_4),
        "w_e0": np.concatenate([np.asarray(L0_gnn_W_edge).T, np.asarray(L0_gnn_b_edge)[None]]),
        "eps": np.asarray(L0_gnn_eps).reshape(1, 1),
        "w1": np.asarray(L0_gnn_W1).T, "b1": column(L0_gnn_b1),
        "w2": np.concatenate([np.asarray(L0_gnn_W2).T, np.asarray(L0_gnn_b2)[None]]),
        "w_node": np.asarray(L1_gnn_W_node), "b_node": column(L1_gnn_b_node),
        "w_ef": np.asarray(L1_gnn_W_edge), "b_ef": column(L1_gnn_b_edge),
        "w_msg": np.asarray(L1_gnn_W_msg).reshape(3, C, C), "b_msg": np.asarray(L1_gnn_b_msg).reshape(1, C),
        "bn_gb": np.concatenate([column(a) for a in (L1_gnn_g_node, L1_gnn_beta_node, L1_gnn_g_edge, L1_gnn_beta_edge,
                                                     L1_gnn_g_msg, L1_gnn_beta_msg)], axis=1),
    }
    arrays = {n: np.ascontiguousarray(a) for n, a in arrays.items()}

    nc = bacc.Bacc("TRN2", target_bir_lowering=False, num_devices=1, dynamic_dma_scratch_size=4096)
    d = {n: nc.dram_tensor(f"in_{n}", a.shape, mybir.dt.from_np(a.dtype), kind="ExternalInput").ap()
         for n, a in arrays.items()}
    d["agg0"] = nc.dram_tensor("agg0", (P, TILES, C1), FP32, kind="Internal").ap()
    d["agg1"] = nc.dram_tensor("agg1", (P, TILES, C), FP32, kind="Internal").ap()
    d["h1"] = nc.dram_tensor("h1", (P, TILES, C), FP32, kind="Internal").ap()
    d["uT"] = nc.dram_tensor("uT", (UROWS, NT * P), FP32, kind="Internal").ap()
    d["out"] = nc.dram_tensor("out", (P, NT, C), FP32, kind="ExternalOutput").ap()
    gnn_kernel(nc, d)
    got = run_bass_kernel_spmd(nc, [{f"in_{n}": a for n, a in arrays.items()}], core_ids=[0]).results[0]["out"]
    return np.asarray(got).transpose(1, 0, 2).reshape(NT * P, C)[:NODES]
```

```python
from contextlib import ExitStack

import concourse.bass as bass
from concourse import mybir

FP32 = mybir.dt.float32
BF16 = mybir.dt.bfloat16
INT32 = mybir.dt.int32
ALU = mybir.AluOpType
ACT = mybir.ActivationFunctionType
AX = mybir.AxisListType

P = 128
NODES, EDGES, C, CE = 50000, 25000, 96, 4
LN_EPS = BN_EPS = 1e-5
G = 4
W = G * P
NT = -(-NODES // W) * G
NG = NT // G
ET = -(-EDGES // P)
EG = ET // G
TILES = NT + 1
DUMP = NT - 1
EDGES_LAST = EDGES - (ET - 1) * P
EW_LAST = EDGES - (EG - 1) * W
NW_LAST = NODES - (NG - 1) * W
assert ET % G == 0 and G == 4 and DUMP * P >= NODES and NG == 2 * EG
C1 = C + 1
ZN = 36
ZW = TILES * C // ZN
assert ZN * ZW == TILES * C

START = 8


def done(g):
    return g + 1 + START


def ago(g, n):
    return g + 1 + START - n


def landed(turn):
    return 16 * (turn + 1)


def pairs_landed(g, pair=0):
    return 16 * (g * 2 + pair)


class Step:

    def __init__(self, it, pos, unroll, count=None, part=None):
        self.it, self.pos, self.unroll, self.count, self.part = it, pos, unroll, count, part

    def group(self, lag):
        return self.it * self.unroll + (self.pos - lag)

    def slot(self, lag, depth=2):
        return (self.pos - lag) % depth

    def turn(self, lag, depth=2):
        return self.it * (self.unroll // depth) + (self.pos - lag) // depth

    def live(self, lag):
        return self.count is None or 0 <= self.group(lag) < self.count

    def last(self, lag):
        return self.count is not None and self.group(lag) == self.count - 1

    def again(self, lag, n=2):
        return self.count is None or self.group(lag) >= n


def run_steps(eng, count, lag, step, unroll):
    first, last = lag // unroll + 1, count // unroll
    for t in range(first * unroll):
        step(Step(t // unroll, t % unroll, unroll, count))
    with eng.Fori(first, last) as it:
        for pos in range(unroll):
            step(Step(it, pos, unroll))
    for t in range(last * unroll, count + lag):
        step(Step(t // unroll, t % unroll, unroll, count))


def settle_waits(eng, mark):
    eng.sem_inc(mark, 1)


class Phase:

    def __init__(self, nc, name):
        self.nc, self.name, self.stack = nc, name, ExitStack()
        self.counts = []

    def __enter__(self):
        self.stack.__enter__()
        return self

    def __exit__(self, *a):
        return self.stack.__exit__(*a)

    def sb(self, name, shape, dt=FP32):
        return self.stack.enter_context(self.nc.sbuf_tensor(f"{self.name}_{name}", shape, dt))

    def ps(self, name, shape, dt=FP32):
        return self.stack.enter_context(self.nc.psum_tensor(f"{self.name}_ps_{name}", shape, dt))

    def sem(self, name):
        return self.stack.enter_context(self.nc.semaphore(f"{self.name}_{name}"))

    def sems(self, name, n=2):
        return [self.sem(f"{name}{i}") for i in range(n)]

    def count(self, name):
        s = self.sem(name)
        self.counts.append(s)
        return s

    def prime(self, eng):
        for s in self.counts:
            eng.sem_inc(s, START)


class Kept:
    pass


def span(start, n):
    return slice(start, start + n) if isinstance(start, int) else bass.ds(start, n)


def tiles(g, n=G):
    return span(g * G, n)


def per_tile(a):
    return a.rearrange("p (t o) -> p t o", o=1).broadcast_to([P, a.shape[1], C])


def edge_phase_0(nc, d, k):
    with Phase(nc, "e0") as ph:
        xs = ph.sb("xs", [P, 4, G, C])
        eaT = ph.sb("eaT", [C1, 2, W])
        ea4T = ph.sb("ea4T", [CE, 2, W])
        dr = ph.sb("dst_row", [P, 2, W], INT32)
        h = ph.sb("h", [P, 2, G, C])
        msg = ph.sb("msg", [P, 2, G, C])
        efT = ph.sb("efT", [C, 2, W])
        S = ph.sb("same_dst", [P, 2, G, 2 * P])
        tot = ph.sb("tot", [P, 2, G, C])
        junk = ph.sb("junk", [P, G, 2 * P], BF16)
        first = ph.sb("first_mask", [P, 2, 2 * P])
        bn = ph.sb("bn", [P, 2, 3 * G, 2, 3])
        mean2 = ph.sb("mean2", [P, 2, 3 * G])
        dif = ph.sb("dif", [P, 2, 3 * G])
        sq = ph.sb("squares", [P, 2, 3 * G])
        dif2 = ph.sb("dif2", [P, 2, 3 * G])
        var4 = ph.sb("var4", [P, 2, 3 * G])
        sd = ph.sb("std", [P, 2, 3 * G])
        rs = ph.sb("rstd", [P, 2, 3 * G])
        nb = ph.sb("nbias", [P, 2, G])
        earlier = ph.sb("earlier", [P, 2, G])
        dup = ph.sb("dup", [P, 2, G])
        shift = ph.sb("shift", [P, 2, G])
        srci = ph.sb("src_i", [P, ET], INT32)
        dsti = ph.sb("dst_i", [P, ET], INT32)
        lo = ph.sb("lo", [P, ET], INT32)
        hi = ph.sb("hi", [P, ET], INT32)
        dump = ph.sb("dump_less_row", [P, ET])
        dumpi = ph.sb("dump_i", [P, G], INT32)
        dumpf = ph.sb("dump_f", [P, G])
        gidx = ph.sb("gather_idx", [P, 4, G], INT32)
        sidx = ph.sb("scatter_idx", [P, 2, G], INT32)
        zero = ph.sb("zero", [P, ZW])
        ps_pre = [ph.ps(f"pre{s}", [P, G, C]) for s in range(2)]
        ps_tot = [ph.ps(f"tot{s}", [P, G, C]) for s in range(2)]
        ps_ef = [ph.ps(f"ef{s}", [C, W]) for s in range(2)]

        const_in, idx_in = ph.sem("const_in"), ph.sem("idx_in")
        zero_made, agg0_zeroed = ph.sem("zero_made"), ph.sem("agg0_zeroed")
        masks_made, masks_filled = ph.sem("masks_made"), ph.sem("masks_filled")
        rows_made, ones_made = ph.sem("rows_made"), ph.sem("ones_made")
        ea_in, ea4_in, dr_in, x_in = (ph.sems(n) for n in ("ea_in", "ea4_in", "dr_in", "x_in"))
        xs_in, scattered = ph.sems("xs_in", 4), ph.sems("scattered")
        gidx_made = ph.count("gidx_made")
        bn_made, halves_made, dif2_made, var_made = (ph.count(n) for n in ("bn_made", "halves_made", "dif2_made", "var_made"))
        std_made, rs_made, nb_made = ph.count("std_made"), ph.count("rs_made"), ph.count("nb_made")
        h_made, msg_made = ph.count("h_made"), ph.count("msg_made")
        S_made, earlier_made, dup_made = ph.count("S_made"), ph.count("earlier_made"), ph.count("dup_made")
        shift_made, srow_made, sidx_made = ph.count("shift_made"), ph.count("srow_made"), ph.count("sidx_made")
        pre_made, ef_made, tot_made = ph.count("pre_made"), ph.count("ef_made"), ph.count("tot_made")
        efr_made, efst_made, tot_out = ph.count("efr_made"), ph.count("efst_made"), ph.count("tot_out")

        xrows = d["x"].rearrange("p t c -> (p t) c")
        aggrows = d["agg0"].rearrange("p t c -> (p t) c")
        LAG = 6

        def steps(eng, step):
            run_steps(eng, EG, LAG, step, 4)

        with nc.Block() as block:

            @block.sync
            def _(sp):
                flat = d["agg0"].rearrange("p t c -> p (t c)")

                def zeros(first, end):
                    with sp.Fori(first, end) as i:
                        sp.dma_start(flat[:, bass.ds(i * ZW, ZW)], zero[:, :]).then_inc(agg0_zeroed, 16)

                sp.dma_start(srci[:, :], d["src_col"]).then_inc(idx_in, 16)
                sp.dma_start(dsti[:, :], d["dst_col"]).then_inc(idx_in, 16)
                sp.dma_start(k.one_eps[:, :], d["eps"].broadcast_to([P, 1])).then_inc(idx_in, 16)
                sp.wait_ge(zero_made, 1)
                zeros(0, 4)
                for to, of in ((k.w_e0[:, :], d["w_e0"]), (k.w_ef[:, :], d["w_ef"]), (k.b_ef[:, :], d["b_ef"]),
                               (k.w1[:, :], d["w1"]), (k.b1[:, :], d["b1"]), (k.w2[:, :], d["w2"]),
                               (k.w_node[:, :], d["w_node"]), (k.b_node[:, :], d["b_node"]),
                               (k.w_msg[:, :, :], d["w_msg"].rearrange("a i o -> i a o")),
                               (k.b_msg[C:C1, :], d["b_msg"]), (k.bn_gb[:, :], d["bn_gb"])):
                    sp.dma_start(to, of).then_inc(const_in, 16)

                def step(t):
                    if t.live(0):
                        g, s = t.group(0), t.slot(0)
                        sp.wait_ge(ef_made, ago(g, 2))
                        sp.dma_start(ea4T[:, s, :], d["ea4T"][:, span(g * W, W)]).then_inc(ea4_in[s], 16)
                        sp.wait_ge(bn_made, ago(g, 2))
                        sp.dma_start(k.R[:, span(g * 2 * G, 2 * G), :], d["x"][:, span(g * 2 * G, 2 * G), :]).then_inc(x_in[s], 16)
                    if t.live(2):
                        g, s = t.group(2), t.slot(2)
                        sp.wait_ge(pre_made, ago(g, 2))
                        sp.dma_start(eaT[0:C, s, :], d["eaT"][:, span(g * W, W)]).then_inc(ea_in[s], 16)
                        sp.wait_ge(earlier_made, ago(g, 2))
                        sp.dma_start(dr[:, s, :], d["dst_row"][:, span(g * W, W)].broadcast_to([P, W])).then_inc(dr_in[s], 16)

                step(Step(0, 0, 4, EG))
                zeros(4, 8)
                step(Step(0, 1, 4, EG))
                for t in range(2, 6):
                    zeros(8 + (t - 2) * (ZN - 8) // 4, 8 + (t - 1) * (ZN - 8) // 4)
                    step(Step(t // 4, t % 4, 4, EG))
                for t in range(6, 8):
                    step(Step(t // 4, t % 4, 4, EG))
                with sp.Fori(2, EG // 4) as it:
                    for pos in range(4):
                        step(Step(it, pos, 4))
                for t in range(EG // 4 * 4, EG + 2):
                    step(Step(t // 4, t % 4, 4, EG))

            @block.gpsimd
            def _(pool):
                ph.prime(pool)
                pool.memset(zero[:, :], 0.0).then_inc(zero_made, 1)
                pool.memset(k.ident[:, :], 0.0).then_inc(masks_filled, 1)
                pool.memset(first[:, :, :], 1.0).then_inc(masks_filled, 1)
                pool.wait_ge(masks_filled, 2)
                pool.affine_select(out=k.ident[:, :], in_=k.ident[:, :], compare_op=ALU.not_equal, fill=1.0,
                                   base=0, pattern=[[-1, P]], channel_multiplier=1).then_inc(masks_made, 1)
                for u in range(2):
                    pool.affine_select(out=first[:, u, :], in_=first[:, u, :], compare_op=ALU.is_gt, fill=0.0,
                                       base=u * P, pattern=[[-1, 2 * P]], channel_multiplier=1).then_inc(masks_made, 1)
                for u in range(2):
                    pool.iota(dumpi[:, u:G:2], pattern=[[0, G // 2]], base=DUMP + u, channel_multiplier=TILES).then_inc(masks_made, 1)

                def gather(t, j):
                    s = t.slot(0, 4)
                    if j == 0:
                        pool.wait_ge(gidx_made, done(t.group(0)))
                        pool.wait_ge(h_made, ago(t.group(0), 4))
                        settle_waits(pool, k.pool_mark)
                    pool.indirect_dma_start(out=xs[:, s, j, :], out_offset=None, in_=xrows,
                                            in_offset=bass.IndirectOffsetOnAxis(ap=gidx[:, s, j:j + 1], axis=0)).then_inc(xs_in[s], 16)

                def scatter(t, j):
                    g = t.group(6)
                    if j == 0:
                        pool.wait_ge(tot_out, done(g))
                        pool.wait_ge(sidx_made, done(g))
                        if not t.again(6, 1):
                            pool.wait_ge(agg0_zeroed, 16 * ZN)
                    if j == 2 or j == 0 and t.again(6, 1):
                        for u in range(2):
                            pool.wait_ge(scattered[u], pairs_landed(g, j // 2))
                        settle_waits(pool, k.pool_mark)
                    pool.indirect_dma_start(out=aggrows, out_offset=bass.IndirectOffsetOnAxis(ap=sidx[:, t.slot(6), j:j + 1], axis=0),
                                            in_=tot[:, t.slot(6), j, :], in_offset=None, compute_op=ALU.add,
                                            bounds_check=P * TILES - 1, oob_is_err=True).then_inc(scattered[j % 2], 16)

                def step(t):
                    for half in range(2):
                        if t.live(6):
                            for j in (2 * half, 2 * half + 1):
                                scatter(t, j)
                        if t.live(0):
                            for j in (2 * half, 2 * half + 1):
                                gather(t, j)

                steps(pool, step)
                for u in range(2):
                    pool.wait_ge(scattered[u], pairs_landed(EG))

            @block.vector
            def _(dve):
                V = nc.vector
                V.memset(eaT[C:C1, :, :], 1.0).then_inc(ones_made, 1)
                dve.wait_ge(idx_in, 16 * 3)
                n = 0
                for of, to in ((srci, k.src_row), (dsti, k.dst_row)):
                    V.tensor_scalar(lo[:, :], of[:, :], P - 1, None, ALU.bitwise_and).then_inc(rows_made, 1)
                    V.tensor_scalar(hi[:, :], of[:, :], 7, None, ALU.logical_shift_right).then_inc(rows_made, 1)
                    dve.wait_ge(rows_made, n + 2)
                    V.scalar_tensor_tensor(to[:, :], lo[:, :], float(TILES), hi[:, :], ALU.mult, ALU.add).then_inc(rows_made, 1)
                    n += 3
                    dve.wait_ge(rows_made, n)
                V.tensor_copy(k.dst_f[:, :], dsti[:, :])
                dve.wait_ge(masks_made, 5)
                V.tensor_copy(dumpf[:, :], dumpi[:, :]).then_inc(rows_made, 1)
                dve.wait_ge(rows_made, n + 1)
                V.tensor_tensor(dump[:, :].rearrange("p (g j) -> p g j", j=G),
                                dumpf[:, :].rearrange("p (o j) -> p o j", o=1).broadcast_to([P, EG, G]),
                                k.dst_row[:, :].rearrange("p (g j) -> p g j", j=G), ALU.subtract).then_inc(rows_made, 1)
                V.tensor_scalar(k.one_eps[:, :], k.one_eps[:, :], 1.0, None, ALU.add)
                V.memset(k.ln_eps[:, :], LN_EPS).then_inc(rows_made, 1)
                dve.wait_ge(rows_made, n + 3)

                def step(t):
                    if t.live(-1):
                        V.tensor_copy(gidx[:, t.slot(-1, 4), :], k.src_row[:, tiles(t.group(-1))]).then_inc(gidx_made, 1)
                    if t.live(3):
                        g, s = t.group(3), t.slot(3)
                        dve.wait_ge(std_made, done(g))
                        V.reciprocal(rs[:, s, :], sd[:, s, :]).then_inc(rs_made, 1)
                        dve.wait_ge(rs_made, done(g))
                        V.scalar_tensor_tensor(nb[:, s, :], mean2[:, s, 0:G], -0.5, rs[:, s, 0:G], ALU.mult, ALU.mult).then_inc(nb_made, 1)
                        V.tensor_scalar(k.mean[:, span(g * 2 * G, 2 * G)], mean2[:, s, G:3 * G], 0.5, None, ALU.mult)
                        V.tensor_scalar(k.rstd[:, span(g * 2 * G, 2 * G)], rs[:, s, G:3 * G], k.one_eps[:, :], None, ALU.mult)
                        dve.wait_ge(efr_made, done(g))
                        V.bn_stats(k.ef_bn[:, span(g, 1), :], efT[:, s, 0:EW_LAST if t.last(3) else W]).then_inc(efst_made, 1)
                    if t.live(2):
                        g, s = t.group(2), t.slot(2)
                        dve.wait_ge(x_in[s], landed(t.turn(2)))
                        dve.wait_ge(xs_in[t.slot(2, 4)], 16 * G * (t.turn(2, 4) + 1))
                        for j in range(G):
                            V.bn_stats(bn[:, s, j, :, :], xs[:, t.slot(2, 4), j, :])
                        for j in range(2 * G):
                            last = V.bn_stats(bn[:, s, G + j, :, :], k.R[:, span(g * 2 * G + j, 1), :])
                        last.then_inc(bn_made, 1)
                    if t.live(4):
                        g, s = t.group(4), t.slot(4)
                        dve.wait_ge(dr_in[s], landed(t.turn(4)))
                        dve.wait_ge(tot_made, ago(g, 2))
                        for j in range(G):
                            pair = dr[:, s, (j // 2) * 2 * P:(j // 2 + 1) * 2 * P]
                            last = V.tensor_scalar(S[:, s, j, :], pair, k.dst_f[:, span(g * G + j, 1)], None, ALU.is_equal)
                        last.then_inc(S_made, 1)
                    if t.live(5):
                        g, s = t.group(5), t.slot(5)
                        dve.wait_ge(srow_made, done(g))
                        if t.again(5):
                            for u in range(2):
                                dve.wait_ge(scattered[u], pairs_landed(g - 1))
                        settle_waits(dve, k.dve_mark)
                        V.tensor_copy(sidx[:, s, :], k.scatter_row[:, tiles(g)]).then_inc(sidx_made, 1)
                    if t.live(2):
                        g, s = t.group(2), t.slot(2)
                        dve.wait_ge(bn_made, done(g))
                        V.tensor_tensor(mean2[:, s, :], bn[:, s, :, 0, 1], bn[:, s, :, 1, 1], ALU.add)
                        V.tensor_tensor(dif[:, s, :], bn[:, s, :, 0, 1], bn[:, s, :, 1, 1], ALU.subtract)
                        V.tensor_tensor(sq[:, s, :], bn[:, s, :, 0, 2], bn[:, s, :, 1, 2], ALU.add).then_inc(halves_made, 1)
                        dve.wait_ge(halves_made, done(g))
                        V.tensor_tensor(dif2[:, s, :], dif[:, s, :], dif[:, s, :], ALU.mult).then_inc(dif2_made, 1)
                        dve.wait_ge(dif2_made, done(g))
                        V.scalar_tensor_tensor(var4[:, s, :], sq[:, s, :], 4.0 / C, dif2[:, s, :], ALU.mult, ALU.add).then_inc(var_made, 1)
                    if t.live(4):
                        g, s = t.group(4), t.slot(4)
                        for j in range(G):
                            n = (j % 2 + 1) * P
                            at = (j // 2) * 2 * P
                            last = V.scalar_tensor_tensor(junk[:, j, 0:n], dr[:, s, at:at + n], k.dst_f[:, span(g * G + j, 1)],
                                                          first[:, j % 2, 0:n], ALU.is_equal, ALU.mult, accum_out=earlier[:, s, j:j + 1])
                        last.then_inc(earlier_made, 1)
                        dve.wait_ge(earlier_made, done(g))
                        V.tensor_scalar(dup[:, s, :], earlier[:, s, :], 0.0, None, ALU.is_gt).then_inc(dup_made, 1)
                        dve.wait_ge(dup_made, done(g))
                        V.tensor_tensor(shift[:, s, :], dup[:, s, :], dump[:, tiles(g)], ALU.mult).then_inc(shift_made, 1)
                        dve.wait_ge(shift_made, done(g))
                        V.tensor_tensor(k.scatter_row[:, tiles(g)], shift[:, s, :], k.dst_row[:, tiles(g)], ALU.add).then_inc(srow_made, 1)

                V.tensor_copy(gidx[:, 0, :], k.src_row[:, tiles(0)]).then_inc(gidx_made, 1)
                steps(dve, step)

            @block.scalar
            def _(act):
                A = nc.scalar
                act.wait_ge(const_in, 16 * 11)
                act.wait_ge(rows_made, 9)

                def step(t):
                    if t.live(4):
                        g, s = t.group(4), t.slot(4)
                        act.wait_ge(pre_made, done(g))
                        act.wait_ge(tot_made, ago(g, 2))
                        A.activation(msg[:, s, :, :], ps_pre[s][:, :, :], ACT.Relu).then_inc(msg_made, 1)
                    if t.live(3):
                        g, s = t.group(3), t.slot(3)
                        act.wait_ge(nb_made, done(g))
                        act.wait_ge(pre_made, ago(g, 2))
                        for j in range(G):
                            last = A.activation(h[:, s, j, :], xs[:, t.slot(3, 4), j, :], ACT.Relu, bias=nb[:, s, j:j + 1], scale=rs[:, s, j:j + 1])
                        last.then_inc(h_made, 1)
                    if t.live(2):
                        g, s = t.group(2), t.slot(2)
                        act.wait_ge(ef_made, done(g))
                        act.wait_ge(efst_made, ago(g, 2))
                        A.activation(efT[:, s, :], ps_ef[s][:, :], ACT.Relu, bias=k.b_ef[:, :]).then_inc(efr_made, 1)
                        act.wait_ge(var_made, done(g))
                        act.wait_ge(rs_made, ago(g, 2))
                        A.activation(sd[:, s, :], var4[:, s, :], ACT.Sqrt, bias=k.ln_eps[:, :], scale=0.25).then_inc(std_made, 1)
                    if t.live(5):
                        g, s = t.group(5), t.slot(5)
                        act.wait_ge(tot_made, done(g))
                        if t.again(5):
                            for u in range(2):
                                act.wait_ge(scattered[u], pairs_landed(g - 1))
                        A.copy(tot[:, s, :, :], ps_tot[s][:, :, :]).then_inc(tot_out, 1)

                steps(act, step)

            @block.tensor
            def _(pe):
                T = nc.tensor
                pe.wait_ge(const_in, 16 * 11)
                pe.wait_ge(masks_made, 5)
                pe.wait_ge(ones_made, 1)

                def step(t):
                    if t.live(4):
                        g, s = t.group(4), t.slot(4)
                        pe.wait_ge(ea_in[s], landed(t.turn(4)))
                        pe.wait_ge(msg_made, ago(g, 2))
                        pe.wait_ge(h_made, done(g))
                        for j in range(G):
                            T.matmul(ps_pre[s][:, j, :], eaT[:, s, j * P:(j + 1) * P], k.w_e0[:, :], start=True, stop=False)
                            last = T.matmul(ps_pre[s][:, j, :], k.ident[:, :], h[:, s, j, :], start=False, stop=True)
                        last.then_inc(pre_made, 1)
                    if t.live(2):
                        g, s = t.group(2), t.slot(2)
                        pe.wait_ge(ea4_in[s], landed(t.turn(2)))
                        pe.wait_ge(efr_made, ago(g, 2))
                        T.matmul(ps_ef[s][:, :], k.w_ef[:, :], ea4T[:, s, :], start=True, stop=True).then_inc(ef_made, 1)
                    if t.live(5):
                        g, s = t.group(5), t.slot(5)
                        pe.wait_ge(S_made, done(g))
                        pe.wait_ge(msg_made, done(g))
                        pe.wait_ge(tot_out, ago(g, 2))
                        for j in range(G):
                            for u in range(2):
                                i = j // 2 * 2 + u
                                last = T.matmul(ps_tot[s][:, j, :], S[:, s, i, (j % 2) * P:(j % 2 + 1) * P], msg[:, s, i, :],
                                                start=(u == 0), stop=(u == 1))
                        last.then_inc(tot_made, 1)

                steps(pe, step)


def node_phase(nc, d, k):
    with Phase(nc, "n0") as ph:
        h0 = ph.sb("h0", [P, 2, G, C])
        agg = ph.sb("agg", [P, 4, G, C])
        hhT = ph.sb("hhT", [C, 2, W])
        r1T = ph.sb("r1T", [C1, 2, W])
        bn = ph.sb("bn", [P, 2, G, 6])
        mv = ph.sb("mean_var", [P, 4, G, 2])
        sd = ph.sb("std", [P, 2, G])
        rs = ph.sb("rstd", [P, 4, G])
        nb = ph.sb("nbias", [P, 2, G])
        h1 = ph.sb("h1", [P, 4, G, C])
        zero = ph.sb("zero", [P, 2 * G, C1])
        efmv = ph.sb("ef_mean_var", [C, 2])
        efsd = ph.sb("ef_std", [C, 1])
        efa = ph.sb("ef_scale", [C, 1])
        fold = ph.sb("ef_fold", [C, C1])
        ps_T = [ph.ps(f"T{s}", [C, W]) for s in range(2)]
        ps_1 = [ph.ps(f"w1{s}", [C, W]) for s in range(2)]
        ps_2 = [ph.ps(f"w2{s}", [P, G, C]) for s in range(2)]
        ps_f = ph.ps("fold", [C1, C])

        setup = ph.sem("setup")
        std_ef, fold_made, zero_made, ones_made = (ph.sem(n) for n in ("std_ef", "fold_made", "zero_made", "ones_made"))
        agg_in, h1_out = ph.sems("agg_in", 4), ph.sems("h1_out", 4)
        agg1_zeroed = ph.sem("agg1_zeroed")
        less_made, h0_made, hh_made = ph.count("less_made"), ph.count("h0_made"), ph.count("hh_made")
        T_made, hhT_made, w1_made, r1_made = (ph.count(n) for n in ("T_made", "hhT_made", "w1_made", "r1_made"))
        w2_made, x1_made, bn_made, mv_made = (ph.count(n) for n in ("w2_made", "x1_made", "bn_made", "mv_made"))
        std_made, rs_made, nb_made = ph.count("std_made"), ph.count("rs_made"), ph.count("nb_made")
        relu_made, less1_made, h1_made = (ph.count(n) for n in ("relu_made", "less1_made", "h1_made"))
        AT = G - 1
        LAG = 13

        def steps(eng, step):
            run_steps(eng, NG, LAG, step, 8)

        with nc.Block() as block:

            @block.sync
            def _(sp):
                sp.wait_ge(zero_made, 1)
                sp.dma_start(d["agg1"][:, NT:TILES, :], zero[:, 0:TILES - NT, :]).then_inc(agg1_zeroed, 16)
                sp.dma_start(d["h1"][:, NT:TILES, :], zero[:, 0:TILES - NT, 0:C]).then_inc(agg1_zeroed, 16)

                def step(t):
                    if t.live(13):
                        g, s = t.group(13), t.slot(13, 4)
                        sp.wait_ge(relu_made, done(g))
                        sp.wait_ge(h1_made, done(g))
                        sp.dma_start(d["h1"][:, tiles(g), :], h1[:, s, :, :]).then_inc(h1_out[s], 16)
                    if t.live(0):
                        g, s = t.group(0), t.slot(0, 4)
                        sp.wait_ge(T_made, ago(g, 4))
                        sp.dma_start(agg[:, s, :, :], d["agg0"][:, tiles(g), :]).then_inc(agg_in[s], 16)
                        if t.pos % 2 == 0:
                            sp.dma_start(d["agg1"][:, tiles(g, 2 * G), :], zero[:, :, :]).then_inc(agg1_zeroed, 16)

                steps(sp, step)
                sp.wait_ge(agg1_zeroed, 16 * (NG // 2 + 2))
                for s in range(4):
                    sp.wait_ge(h1_out[s], landed(-(-(NG - s) // 4)))

            @block.gpsimd
            def _(pool):
                ph.prime(pool)
                for out in h1_out:
                    pool.sem_inc(out, 16)
                pool.memset(zero[:, :, :], 0.0).then_inc(zero_made, 1)

                def step(t):
                    if t.live(11):
                        g, s = t.group(11), t.slot(11, 4)
                        pool.wait_ge(mv_made, done(g))
                        pool.wait_ge(h1_out[s], landed(t.turn(11, 4)))
                        pool.tensor_tensor(h1[:, s, AT:G, :], k.R[:, span(g * G + AT, 1), :], per_tile(mv[:, s, AT:G, 0]), ALU.subtract).then_inc(less1_made, 1)
                    if t.live(2):
                        g, s = t.group(2), t.slot(2, 4)
                        pool.wait_ge(h0_made, done(g))
                        pool.wait_ge(agg_in[s], landed(t.turn(2, 4)))
                        pool.tensor_tensor(agg[:, s, :, :], h0[:, t.slot(2), :, :], agg[:, s, :, :], ALU.add).then_inc(hh_made, 1)
                    if t.live(0):
                        g, s = t.group(0), t.slot(0)
                        pool.wait_ge(hh_made, ago(g, 2))
                        pool.tensor_tensor(h0[:, s, :, :], k.R[:, tiles(g), :], per_tile(k.mean[:, tiles(g)]), ALU.subtract).then_inc(less_made, 1)

                steps(pool, step)

            @block.scalar
            def _(act):
                A = nc.scalar
                act.wait_ge(setup, 1)
                A.activation(efsd[:, :], efmv[:, 1:2], ACT.Sqrt, bias=k.ln_eps[0:C, :]).then_inc(std_ef, 1)
                act.wait_ge(ones_made, 1)

                def step(t):
                    if t.live(9):
                        g, s = t.group(9), t.slot(9)
                        act.wait_ge(mv_made, done(g))
                        act.wait_ge(rs_made, ago(g, 2))
                        A.activation(sd[:, s, :], mv[:, t.slot(9, 4), :, 1], ACT.Sqrt, bias=k.ln_eps[:, :]).then_inc(std_made, 1)
                    if t.live(11):
                        g, s = t.group(11), t.slot(11)
                        act.wait_ge(nb_made, done(g))
                        act.wait_ge(h1_out[t.slot(11, 4)], landed(t.turn(11, 4)))
                        for j in range(AT):
                            last = A.activation(h1[:, t.slot(11, 4), j, :], k.R[:, span(g * G + j, 1), :], ACT.Relu,
                                                bias=nb[:, s, j:j + 1], scale=rs[:, t.slot(11, 4), j:j + 1])
                        last.then_inc(relu_made, 1)
                    if t.live(4):
                        g, s = t.group(4), t.slot(4)
                        act.wait_ge(T_made, done(g))
                        act.wait_ge(w1_made, ago(g, 2))
                        A.copy(hhT[:, s, :], ps_T[s][:, :]).then_inc(hhT_made, 1)
                    if t.live(6):
                        g, s = t.group(6), t.slot(6)
                        act.wait_ge(w1_made, done(g))
                        act.wait_ge(w2_made, ago(g, 2))
                        A.activation(r1T[0:C, s, :], ps_1[s][:, :], ACT.Relu, bias=k.b1[:, :]).then_inc(r1_made, 1)

                steps(act, step)

            @block.vector
            def _(dve):
                V = nc.vector
                V.memset(r1T[C:C1, :, :], 1.0).then_inc(ones_made, 1)
                V.bn_aggr(efmv[:, :], k.ef_bn[:, :, :]).then_inc(setup, 1)
                dve.wait_ge(std_ef, 1)
                V.reciprocal(efa[:, :], efsd[:, :]).then_inc(setup, 1)
                dve.wait_ge(setup, 2)
                V.tensor_tensor(efa[:, :], efa[:, :], k.bn_gb[:, 2:3], ALU.mult).then_inc(setup, 1)
                dve.wait_ge(setup, 3)
                V.tensor_scalar(fold[:, 0:C], k.ident[0:C, 0:C], efa[:, :], None, ALU.mult)
                V.tensor_tensor(fold[:, C:C1], efmv[:, 0:1], efa[:, :], ALU.mult).then_inc(setup, 1)
                dve.wait_ge(setup, 4)
                V.tensor_tensor(fold[:, C:C1], k.bn_gb[:, 3:4], fold[:, C:C1], ALU.subtract).then_inc(setup, 1)
                dve.wait_ge(fold_made, 1)
                V.tensor_copy(k.w_ef_msg[0:C, :], ps_f[0:C, :])
                V.tensor_tensor(k.w_ef_msg[C:C1, :], ps_f[C:C1, :], k.b_msg[C:C1, :], ALU.add)

                def step(t):
                    if t.live(8):
                        g, s = t.group(8), t.slot(8)
                        dve.wait_ge(w2_made, done(g))
                        V.tensor_tensor(k.R[:, tiles(g), :], ps_2[s][:, :, :], k.R[:, tiles(g), :], ALU.add).then_inc(x1_made, 1)
                    if t.live(10):
                        g, s = t.group(10), t.slot(10)
                        dve.wait_ge(std_made, done(g))
                        dve.wait_ge(relu_made, ago(g, 4))
                        V.reciprocal(rs[:, t.slot(10, 4), :], sd[:, s, :]).then_inc(rs_made, 1)
                    if t.live(8):
                        g, s = t.group(8), t.slot(8)
                        dve.wait_ge(x1_made, done(g))
                        settle_waits(dve, k.dve_mark)
                        for j in range(G):
                            last = V.bn_stats(bn[:, s, j, :], k.R[:, span(g * G + j, 1), :])
                        last.then_inc(bn_made, 1)
                    if t.live(10):
                        g, s = t.group(10), t.slot(10)
                        dve.wait_ge(rs_made, done(g))
                        dve.wait_ge(relu_made, ago(g, 2))
                        V.scalar_tensor_tensor(nb[:, s, :], mv[:, t.slot(10, 4), :, 0], -1.0, rs[:, t.slot(10, 4), :], ALU.mult, ALU.mult).then_inc(nb_made, 1)
                    if t.live(12):
                        g, s = t.group(12), t.slot(12, 4)
                        dve.wait_ge(less1_made, done(g))
                        V.tensor_scalar(h1[:, s, AT, :], h1[:, s, AT, :], 0.0, rs[:, s, AT:G], ALU.max, ALU.mult).then_inc(h1_made, 1)
                    if t.live(1):
                        g, s = t.group(1), t.slot(1)
                        dve.wait_ge(less_made, done(g))
                        V.scalar_tensor_tensor(h0[:, s, :, :], h0[:, s, :, :], 0.0, per_tile(k.rstd[:, tiles(g)]), ALU.max, ALU.mult).then_inc(h0_made, 1)
                    if t.live(8):
                        g, s = t.group(8), t.slot(8)
                        dve.wait_ge(bn_made, done(g))
                        dve.wait_ge(relu_made, ago(g, 4))
                        dve.wait_ge(less1_made, ago(g, 4))
                        settle_waits(dve, k.dve_mark)
                        for j in range(G):
                            last = V.bn_aggr(mv[:, t.slot(8, 4), j, :], bn[:, s, j, :])
                        last.then_inc(mv_made, 1)

                steps(dve, step)

            @block.tensor
            def _(pe):
                T = nc.tensor
                pe.wait_ge(setup, 5)
                T.matmul(ps_f[:, :], fold[:, :], k.w_msg[:, 2, :], start=True, stop=True).then_inc(fold_made, 1)
                pe.wait_ge(ones_made, 1)

                def step(t):
                    if t.live(7):
                        g, s = t.group(7), t.slot(7)
                        pe.wait_ge(r1_made, done(g))
                        pe.wait_ge(x1_made, ago(g, 2))
                        for j in range(G):
                            last = T.matmul(ps_2[s][:, j, :], r1T[:, s, j * P:(j + 1) * P], k.w2[:, :], start=True, stop=True)
                        last.then_inc(w2_made, 1)
                    if t.live(3):
                        g, s = t.group(3), t.slot(3)
                        pe.wait_ge(hh_made, done(g))
                        pe.wait_ge(hhT_made, ago(g, 2))
                        for j in range(G):
                            last = T.transpose(ps_T[s][:, j * P:(j + 1) * P], agg[:, t.slot(3, 4), j, :], k.ident[:, :])
                        last.then_inc(T_made, 1)
                    if t.live(5):
                        g, s = t.group(5), t.slot(5)
                        pe.wait_ge(hhT_made, done(g))
                        pe.wait_ge(r1_made, ago(g, 2))
                        T.matmul(ps_1[s][:, :], k.w1[:, :], hhT[0:C, s, :], start=True, stop=True).then_inc(w1_made, 1)

                steps(pe, step)


def edge_phase_1(nc, d, k):
    with Phase(nc, "e1") as ph:
        hs = ph.sb("h_src", [P, 4, G, C])
        hd = ph.sb("h_dst", [P, 4, G, C])
        ea4T = ph.sb("ea4T", [CE, 2, W])
        dr = ph.sb("dst_row", [P, 2, W], INT32)
        hsT = ph.sb("h_srcT", [C, W])
        hdT = ph.sb("h_dstT", [C, W])
        efT = ph.sb("efT", [C1, W])
        msg = ph.sb("msg", [P, 2, G, C1])
        S = ph.sb("same_dst", [P, 2, G, 2 * P])
        tot = ph.sb("tot", [P, 2, G, C1])
        gidx = ph.sb("gather_idx", [P, 4, 2, G], INT32)
        sidx = ph.sb("scatter_idx", [P, 2, G], INT32)
        node_in = ph.sb("node_in", [P, 4, W])
        h1T = ph.sb("h1T", [C, 2, W])
        uT = ph.sb("uT", [C, 4, W])
        st = ph.sb("mean_var", [C, 2])
        sd = ph.sb("std", [C, 1])
        scale = ph.sb("scale", [C, 1])
        fold = ph.sb("fold", [C, C1])
        w_out = ph.sb("w_out", [C1, C])
        nothing = ph.sb("nothing", [P, C1])
        ps_s = ph.ps("sT", [C, W])
        ps_d = ph.ps("dT", [C, W])
        ps_ef = ph.ps("ef", [C, W])
        ps_m = ph.ps("m", [P, G, C])
        ps_tot = ph.ps("tot", [P, G, C1])
        ps_n = [ph.ps(f"node{s}", [P, W]) for s in range(2)]
        ps_hT, ps_u = ps_n[0][0:C, :], ps_n[1][0:C, :]
        ps_gram = ph.ps("gram", [C, C1])

        ones_made, nothing_made = ph.sem("ones_made"), ph.sem("nothing_made")
        ea4_in, dr_in, scattered = (ph.sems(n) for n in ("ea4_in", "dr_in", "scattered"))
        hs_in, hd_in = ph.sems("hs_in", 4), ph.sems("hd_in", 4)
        h1_in, uT_in, uT_out = ph.sems("h1_in", 4), ph.sems("uT_in", 4), ph.sems("uT_out", 4)
        gidx_made, sidx_made, S_made, sT_out, dT_out = (ph.count(n) for n in ("gidx_made", "sidx_made", "S_made", "sT_out", "dT_out"))
        s_made, d_made, ef_made, ef_out = (ph.count(n) for n in ("s_made", "d_made", "ef_made", "ef_out"))
        m_made, msg_made, tot_made, tot_out = (ph.count(n) for n in ("m_made", "msg_made", "tot_made", "tot_out"))
        hT_made, hT_out, u_made, uT_made, ubn_made = (ph.count(n) for n in ("hT_made", "hT_out", "u_made", "uT_made", "ubn_made"))
        sum_made, y_made = ph.count("sum_made"), ph.count("y_made")
        gram_made, aggr_made, std_made, folded, fold_made, w_made, row_made = (
            ph.sem(n) for n in ("gram_made", "aggr_made", "std_made", "folded", "fold_made", "w_made", "row_made"))

        hrows = d["h1"].rearrange("p t c -> (p t) c")
        aggrows = d["agg1"].rearrange("p t c -> (p t) c")
        LAG = 4
        U, Y, Y_AT = 4, 5, 28
        U_END = -(-NG // U) + 1
        assert U_END + 2 <= Y_AT and Y_AT % 4 == 0 and 16 * Y <= NG <= (EG + LAG - Y_AT) * Y

        def steps(eng, step):
            def written_out(first, end):
                for t in range(first, end):
                    step(Step(t // 4, t % 4, 4, EG))

            def loop(first, end, part):
                with eng.Fori(first // 4, end // 4) as it:
                    for pos in range(4):
                        step(Step(it, pos, 4, part=part))

            written_out(0, 8)
            loop(8, 24, "u")
            written_out(24, Y_AT)
            loop(Y_AT, Y_AT + 16, "y")
            written_out(Y_AT + 16, EG + LAG)

        def matmul_lag(v):
            return 2 if v == U - 1 else 1

        def u_group(t, lag, v):
            u = t.group(lag) * U + v
            if t.count is None:
                return u if t.part == "u" else None
            return u if 0 <= u < NG else None

        def y_group(t, lag, v):
            y = (t.group(lag) - Y_AT) * Y + v
            if t.count is None:
                return y if t.part == "y" else None
            return y if 0 <= y < NG else None

        def y_slot(t, lag, v, depth):
            return ((t.pos - lag) * Y + v) % depth

        def y_turn(t, lag, v, depth):
            return t.it * (4 * Y // depth) + ((t.pos - lag) * Y + v) // depth - Y_AT * Y // depth

        with nc.Block() as block:

            @block.sync
            def _(sp):
                def step(t):
                    if t.live(0):
                        g, s = t.group(0), t.slot(0)
                        sp.wait_ge(ef_made, ago(g, 2))
                        sp.dma_start(ea4T[:, s, :], d["ea4T"][:, span(g * W, W)]).then_inc(ea4_in[s], 16)
                        sp.wait_ge(S_made, ago(g, 2))
                        sp.dma_start(dr[:, s, :], d["dst_row"][:, span(g * W, W)].broadcast_to([P, W])).then_inc(dr_in[s], 16)
                    for v in (3, 0, 1, 2):
                        u = u_group(t, matmul_lag(v), v)
                        if u is not None:
                            sp.wait_ge(uT_made, done(u))
                            sp.dma_start(d["uT"][:, span(u * W, W)], uT[:, v, :]).then_inc(uT_out[v], 16)
                        u = u_group(t, 0, v)
                        if u is not None:
                            sp.wait_ge(hT_made, ago(u, 4))
                            sp.dma_start(node_in[:, v, 0:G * C].rearrange("p (t c) -> p t c", c=C), d["h1"][:, tiles(u), :]).then_inc(h1_in[v], 16)
                    for v in range(Y):
                        y = y_group(t, -1, v)
                        if y is not None:
                            if isinstance(y, int) and y == 0:
                                for w in range(4):
                                    sp.wait_ge(uT_out[w], landed(-(-(NG - w) // 4)))
                                sp.wait_ge(row_made, 1)
                            sp.wait_ge(sum_made, ago(y, 4))
                            s = y_slot(t, -1, v, 4)
                            sp.dma_start(node_in[0:C, s, :], d["uT"][:, span(y * W, W)]).then_inc(uT_in[s], 16)

                steps(sp, step)

            @block.gpsimd
            def _(pool):
                ph.prime(pool)
                pool.memset(msg[:, :, :, C:C1], 1.0).then_inc(ones_made, 1)
                pool.memset(nothing[:, :], 0.0).then_inc(nothing_made, 1)
                for v in range(4):
                    pool.sem_inc(uT_out[v], 16)

                def gather(t, j):
                    g, s = t.group(0), t.slot(0, 4)
                    if j == 0:
                        pool.wait_ge(gidx_made, done(g))
                        pool.wait_ge(s_made, ago(g, 4))
                        pool.wait_ge(d_made, ago(g, 4))
                        settle_waits(pool, k.pool_mark)
                    for v, (to, got) in enumerate(((hs, hs_in), (hd, hd_in))):
                        pool.indirect_dma_start(out=to[:, s, j, :], out_offset=None, in_=hrows,
                                                in_offset=bass.IndirectOffsetOnAxis(ap=gidx[:, s, v, j:j + 1], axis=0)).then_inc(got[s], 16)

                def scatter(t, j):
                    g = t.group(4)
                    if j == 0:
                        pool.wait_ge(tot_out, done(g))
                        pool.wait_ge(sidx_made, done(g))
                    if j == 2 or j == 0 and t.again(4, 1):
                        for u in range(2):
                            pool.wait_ge(scattered[u], pairs_landed(g, j // 2))
                        settle_waits(pool, k.pool_mark)
                    pool.indirect_dma_start(out=aggrows, out_offset=bass.IndirectOffsetOnAxis(ap=sidx[:, t.slot(4), j:j + 1], axis=0),
                                            in_=tot[:, t.slot(4), j, :], in_offset=None, compute_op=ALU.add,
                                            bounds_check=P * TILES - 1, oob_is_err=True).then_inc(scattered[j % 2], 16)

                def step(t):
                    for half in range(2):
                        if t.live(0):
                            for j in (2 * half, 2 * half + 1):
                                gather(t, j)
                        if t.live(4):
                            for j in (2 * half, 2 * half + 1):
                                scatter(t, j)

                steps(pool, step)
                for u in range(2):
                    pool.wait_ge(scattered[u], pairs_landed(EG))

            @block.vector
            def _(dve):
                V = nc.vector
                V.memset(efT[C:C1, :], 1.0).then_inc(ones_made, 1)

                def indices(t, lag):
                    g, s = t.group(lag), t.slot(lag, 4)
                    if t.again(lag, 4):
                        dve.wait_ge(hs_in[s], 16 * G * t.turn(lag, 4))
                        dve.wait_ge(hd_in[s], 16 * G * t.turn(lag, 4))
                        settle_waits(dve, k.dve_mark)
                    V.tensor_copy(gidx[:, s, 0, :], k.src_row[:, tiles(g)])
                    V.tensor_copy(gidx[:, s, 1, :], k.dst_row[:, tiles(g)]).then_inc(gidx_made, 1)

                def h1_copy(t, v):
                    u = u_group(t, 1, v)
                    if u is not None:
                        dve.wait_ge(hT_made, done(u))
                        dve.wait_ge(u_made, ago(u, 2))
                        V.tensor_copy(h1T[:, v % 2, :], ps_hT).then_inc(hT_out, 1)

                def u_stats(t, v):
                    u = u_group(t, matmul_lag(v), v)
                    if u is not None:
                        dve.wait_ge(uT_made, done(u))
                        settle_waits(dve, k.dve_mark)
                        cols = NW_LAST if isinstance(u, int) and u == NG - 1 else W
                        V.bn_stats(k.u_bn[:, span(u, 1), :], uT[:, v, 0:cols]).then_inc(ubn_made, 1)

                def add(t, v):
                    y = y_group(t, 0, v)
                    if y is not None:
                        dve.wait_ge(sum_made, done(y))
                        ps = ps_n[y_slot(t, 0, v, 2)][:, 0:G * C].rearrange("p (t c) -> p t c", c=C)
                        V.tensor_tensor(k.R[:, tiles(y), :], ps, k.R[:, tiles(y), :], ALU.add).then_inc(y_made, 1)

                def statistics():
                    dve.wait_ge(ubn_made, done(NG - 1))
                    V.bn_aggr(st[:, :], k.u_bn[:, :, :]).then_inc(aggr_made, 1)
                    dve.wait_ge(hT_made, done(NG - 1))
                    V.memset(node_in[C:C1, :, :], 1.0).then_inc(row_made, 1)

                def batch_norm():
                    dve.wait_ge(std_made, 1)
                    V.reciprocal(scale[:, :], sd[:, :]).then_inc(folded, 1)
                    dve.wait_ge(folded, 1)
                    V.tensor_tensor(scale[:, :], scale[:, :], k.bn_gb[:, 0:1], ALU.mult).then_inc(folded, 1)
                    dve.wait_ge(folded, 2)
                    V.tensor_scalar(fold[:, 0:C], k.ident[0:C, 0:C], scale[:, :], None, ALU.mult)
                    V.tensor_tensor(fold[:, C:C1], st[:, 0:1], scale[:, :], ALU.mult).then_inc(folded, 1)
                    dve.wait_ge(folded, 3)
                    V.tensor_tensor(fold[:, C:C1], k.bn_gb[:, 1:2], fold[:, C:C1], ALU.subtract).then_inc(folded, 1)

                def step(t):
                    if t.count is not None and t.group(0) == 0:
                        indices(t, 0)
                    if t.live(-1):
                        indices(t, -1)
                    if t.count is not None and t.group(0) == Y_AT - 2:
                        statistics()
                    if t.count is not None and t.group(0) == Y_AT - 1:
                        batch_norm()
                    h1_copy(t, 0)
                    add(t, 0)
                    if t.live(2):
                        g, s = t.group(2), t.slot(2)
                        dve.wait_ge(d_made, done(g))
                        dve.wait_ge(m_made, ago(g, 1))
                        V.tensor_copy(hdT[:, :], ps_d[:, :]).then_inc(dT_out, 1)
                    h1_copy(t, 1)
                    add(t, 1)
                    if t.live(2):
                        dve.wait_ge(dr_in[s], landed(t.turn(2)))
                        dve.wait_ge(tot_made, ago(g, 2))
                        for j in range(G):
                            pair = dr[:, s, (j // 2) * 2 * P:(j // 2 + 1) * 2 * P]
                            last = V.tensor_scalar(S[:, s, j, :], pair, k.dst_f[:, span(g * G + j, 1)], None, ALU.is_equal)
                        last.then_inc(S_made, 1)
                    u_stats(t, 3)
                    h1_copy(t, 2)
                    add(t, 2)
                    u_stats(t, 0)
                    if t.live(3):
                        g, s = t.group(3), t.slot(3)
                        if t.again(3):
                            for u in range(2):
                                dve.wait_ge(scattered[u], pairs_landed(g - 1))
                        settle_waits(dve, k.dve_mark)
                        V.tensor_copy(sidx[:, s, :], k.scatter_row[:, tiles(g)]).then_inc(sidx_made, 1)
                    h1_copy(t, 3)
                    add(t, 3)
                    u_stats(t, 1)
                    u_stats(t, 2)
                    add(t, 4)
                    if t.count is not None and t.group(0) == Y_AT - 1:
                        dve.wait_ge(fold_made, 1)
                        V.tensor_copy(w_out[:, :], ps_n[0][0:C1, 0:C]).then_inc(w_made, 1)

                steps(dve, step)
                dve.wait_ge(gram_made, 1)
                V.tensor_copy(k.gram[:, :], ps_gram[:, :])

            @block.scalar
            def _(act):
                A = nc.scalar

                def features(t, v):
                    u = u_group(t, matmul_lag(v), v)
                    if u is not None:
                        act.wait_ge(u_made, done(u))
                        act.wait_ge(ubn_made, ago(u, 4))
                        act.wait_ge(uT_out[v], landed(t.group(matmul_lag(v))))
                        A.activation(uT[:, v, :], ps_u, ACT.Relu, bias=k.b_node[:, :]).then_inc(uT_made, 1)

                def step(t):
                    if t.live(3):
                        g, s = t.group(3), t.slot(3)
                        act.wait_ge(m_made, done(g))
                        act.wait_ge(tot_made, ago(g, 2))
                        A.activation(msg[:, s, :, 0:C], ps_m[:, :, :], ACT.Relu).then_inc(msg_made, 1)
                    features(t, 3)
                    if t.live(2):
                        g = t.group(2)
                        act.wait_ge(s_made, done(g))
                        act.wait_ge(m_made, ago(g, 1))
                        A.copy(hsT[:, :], ps_s[:, :]).then_inc(sT_out, 1)
                        act.wait_ge(ef_made, done(g))
                        A.activation(efT[0:C, :], ps_ef[:, :], ACT.Relu, bias=k.b_ef[:, :]).then_inc(ef_out, 1)
                    features(t, 0)
                    features(t, 1)
                    if t.live(3):
                        g, s = t.group(3), t.slot(3)
                        act.wait_ge(tot_made, done(g))
                        if t.again(3):
                            for w in range(2):
                                act.wait_ge(scattered[w], pairs_landed(g - 1))
                        A.copy(tot[:, s, :, :], ps_tot[:, :, :]).then_inc(tot_out, 1)
                    features(t, 2)
                    if t.count is not None and t.group(0) == Y_AT - 2:
                        act.wait_ge(aggr_made, 1)
                        A.activation(sd[:, :], st[:, 1:2], ACT.Sqrt, bias=k.ln_eps[0:C, :]).then_inc(std_made, 1)

                steps(act, step)

            @block.tensor
            def _(pe):
                T = nc.tensor
                pe.wait_ge(nothing_made, 1)
                pe.wait_ge(ones_made, 2)
                T.matmul(ps_gram[:, :], nothing[:, 0:C], nothing[:, :], start=True, stop=False)

                def transposes(to, of, s, made):
                    for j in range(G):
                        last = T.transpose(to[:, j * P:(j + 1) * P], of[:, s, j, :], k.ident[:, :])
                    last.then_inc(made, 1)

                def sums(s, js):
                    for j in js:
                        for u in range(2):
                            i = j // 2 * 2 + u
                            last = T.matmul(ps_tot[:, j, :], S[:, s, i, (j % 2) * P:(j % 2 + 1) * P], msg[:, s, i, :],
                                            start=(u == 0), stop=(u == 1))
                    return last

                def node_T(t, v):
                    u = u_group(t, 1, v)
                    if u is not None:
                        pe.wait_ge(h1_in[v], landed(t.group(1)))
                        pe.wait_ge(hT_out, ago(u, 1))
                        for j in range(G):
                            last = T.transpose(ps_hT[:, j * P:(j + 1) * P], node_in[:, v, j * C:(j + 1) * C], k.ident[:, :])
                        last.then_inc(hT_made, 1)

                def node_mm(t, v):
                    u = u_group(t, matmul_lag(v), v)
                    if u is not None:
                        pe.wait_ge(hT_out, done(u))
                        pe.wait_ge(uT_made, ago(u, 1))
                        T.matmul(ps_u, k.w_node[:, :], h1T[:, v % 2, :], start=True, stop=True).then_inc(u_made, 1)

                def node_sum(t, v):
                    y = y_group(t, 0, v)
                    if y is not None:
                        s = y_slot(t, 0, v, 4)
                        pe.wait_ge(uT_in[s], landed(y_turn(t, 0, v, 4)))
                        pe.wait_ge(y_made, ago(y, 2))
                        for j in range(G):
                            last = T.matmul(ps_n[y_slot(t, 0, v, 2)][:, j * C:(j + 1) * C], node_in[0:C1, s, j * P:(j + 1) * P], w_out[:, :],
                                            start=True, stop=True)
                        last.then_inc(sum_made, 1)

                def step(t):
                    if t.live(3):
                        g, s = t.group(3), t.slot(3)
                        pe.wait_ge(sT_out, done(g))
                        pe.wait_ge(dT_out, done(g))
                        pe.wait_ge(ef_out, done(g))
                        pe.wait_ge(msg_made, ago(g, 1))
                        for j in range(G):
                            for n, (x, w) in enumerate(((hsT, k.w_msg[:, 0, :]), (hdT, k.w_msg[:, 1, :]), (efT, k.w_ef_msg[:, :]))):
                                last = T.matmul(ps_m[:, j, :], x[:, j * P:(j + 1) * P], w, start=(n == 0), stop=(n == 2))
                        last.then_inc(m_made, 1)
                    node_mm(t, 3)
                    node_T(t, 0)
                    node_sum(t, 0)
                    if t.live(2):
                        g, s = t.group(2), t.slot(2, 4)
                        pe.wait_ge(hs_in[s], 16 * G * (t.turn(2, 4) + 1))
                        pe.wait_ge(sT_out, ago(g, 1))
                        transposes(ps_s, hs, s, s_made)
                        pe.wait_ge(hd_in[s], 16 * G * (t.turn(2, 4) + 1))
                        pe.wait_ge(dT_out, ago(g, 1))
                        transposes(ps_d, hd, s, d_made)
                        pe.wait_ge(ea4_in[t.slot(2)], landed(t.turn(2)))
                        pe.wait_ge(ef_out, ago(g, 1))
                        T.matmul(ps_ef[:, :], k.w_ef[:, :], ea4T[:, t.slot(2), :], start=True, stop=True).then_inc(ef_made, 1)
                    node_mm(t, 0)
                    node_T(t, 1)
                    node_sum(t, 1)
                    if t.count is not None and t.group(0) == Y_AT - 1:
                        pe.wait_ge(folded, 4)
                        T.matmul(ps_n[0][0:C1, 0:C], fold[:, :], k.ident[0:C, 0:C], start=True, stop=True).then_inc(fold_made, 1)
                    if t.live(3):
                        g, s = t.group(3), t.slot(3)
                        pe.wait_ge(msg_made, done(g))
                        for j in range(G):
                            r = EDGES_LAST if j == G - 1 and t.last(3) else P
                            last = T.matmul(ps_gram[:, :], msg[0:r, s, j, 0:C], msg[0:r, s, j, :], start=False, stop=(r < P))
                        if t.last(3):
                            last.then_inc(gram_made, 1)
                        pe.wait_ge(S_made, done(g))
                        pe.wait_ge(tot_out, ago(g, 1))
                        sums(s, (0, 1))
                    node_T(t, 2)
                    node_mm(t, 1)
                    node_sum(t, 2)
                    if t.live(3):
                        sums(s, (2, 3)).then_inc(tot_made, 1)
                    node_T(t, 3)
                    node_sum(t, 3)
                    node_mm(t, 2)
                    node_sum(t, 4)
                    if t.count is not None and t.group(0) == Y_AT - 1:
                        pe.wait_ge(w_made, 1)

                steps(pe, step)


def final_phase(nc, d, k):
    with Phase(nc, "f") as ph:
        agg = ph.sb("agg", [P, 8, G, C1])
        y = ph.sb("y", [P, 8, G, C])
        st = ph.sb("stats", [C, 2])
        tmp = ph.sb("tmp", [C, C])
        mean_sq = ph.sb("mean_squared", [C, 1])
        sd = ph.sb("std", [C, 1])
        scale = ph.sb("scale", [C, 1])
        shift = ph.sb("shift", [C, 1])
        a_col = ph.sb("scale_column", [C, P])
        a_row = ph.sb("scale_row", [P, C])
        c_col = ph.sb("shift_column", [C, P])
        c_row = ph.sb("shift_row", [P, C])
        ps_c = ph.ps("shift_row", [P, C])
        ps_a = ph.ps("scale_row", [P, C])

        setup, std_made, rows_made = (ph.sem(n) for n in ("setup", "std_made", "rows_made"))
        agg_in, y_out = ph.sems("agg_in", 4), ph.sems("y_out", 4)
        scaled, shifts_made, sum_made, y_made = (ph.count(n) for n in ("scaled", "shifts_made", "sum_made", "y_made"))
        SETUP = 9
        LAG = 6

        def steps(eng, step):
            run_steps(eng, NG, LAG, step, 8)

        with nc.Block() as block:

            @block.sync
            def _(sp):
                def step(t):
                    if t.live(6) and t.slot(6, 8) % 2:
                        g, s = t.group(6), t.slot(6, 8)
                        sp.wait_ge(y_made, done(g))
                        sp.dma_start(d["out"][:, tiles(g - 1, 2 * G), :], y[:, s - 1:s + 1, :, :].rearrange("p a t c -> p (a t) c")).then_inc(y_out[s // 2], 16)
                    if t.live(0) and t.slot(0, 8) % 2 == 0:
                        g, s = t.group(0), t.slot(0, 8)
                        sp.wait_ge(sum_made, ago(g + 1, 8))
                        sp.dma_start(agg[:, s:s + 2, :, :].rearrange("p a t c -> p (a t) c"), d["agg1"][:, tiles(g, 2 * G), :]).then_inc(agg_in[s // 2], 16)

                steps(sp, step)
                for s in range(4):
                    sp.wait_ge(y_out[s], landed(-(-(NG // 2 - s) // 4)))

            @block.gpsimd
            def _(pool):
                ph.prime(pool)
                for out in y_out:
                    pool.sem_inc(out, 16)

                def step(t):
                    if t.live(4):
                        g, s = t.group(4), t.slot(4, 8)
                        pool.wait_ge(shifts_made, done(g))
                        pool.wait_ge(scaled, done(g))
                        pool.tensor_tensor(y[:, s, :, :], y[:, s, :, :], agg[:, s, :, 0:C], ALU.add).then_inc(sum_made, 1)

                steps(pool, step)

            @block.vector
            def _(dve):
                V = nc.vector
                n = 0

                def settle(ins):
                    nonlocal n
                    n += 1
                    ins.then_inc(setup, 1)
                    dve.wait_ge(setup, n)

                V.tensor_scalar(st[:, 0:1], k.gram[:, C:C1], 1.0 / EDGES, None, ALU.mult)
                settle(V.tensor_tensor(tmp[:, :], k.gram[:, 0:C], k.ident[0:C, 0:C], ALU.mult))
                settle(V.reduce_sum(sd[:, :], tmp[:, :], AX.X))
                settle(V.tensor_tensor(mean_sq[:, :], st[:, 0:1], st[:, 0:1], ALU.mult))
                settle(V.scalar_tensor_tensor(st[:, 1:2], sd[:, :], 1.0 / EDGES, mean_sq[:, :], ALU.mult, ALU.subtract))
                dve.wait_ge(std_made, 1)
                settle(V.reciprocal(scale[:, :], sd[:, :]))
                settle(V.tensor_tensor(scale[:, :], scale[:, :], k.bn_gb[:, 4:5], ALU.mult))
                settle(V.tensor_tensor(shift[:, :], st[:, 0:1], scale[:, :], ALU.mult))
                settle(V.tensor_tensor(shift[:, :], k.bn_gb[:, 5:6], shift[:, :], ALU.subtract))
                V.tensor_copy(c_col[:, :], shift[:, 0:1].broadcast_to([C, P]))
                settle(V.tensor_copy(a_col[:, :], scale[:, 0:1].broadcast_to([C, P])))
                assert n == SETUP
                dve.wait_ge(rows_made, 1)
                V.tensor_copy(c_row[:, :], ps_c[:, :])
                settle(V.tensor_copy(a_row[:, :], ps_a[:, :]))
                a_rows = a_row[:, :].rearrange("p (o c) -> p o c", o=1).broadcast_to([P, G, C])

                def step(t):
                    if t.live(5):
                        g, s = t.group(5), t.slot(5, 8)
                        dve.wait_ge(sum_made, done(g))
                        V.tensor_tensor(y[:, s, :, :], y[:, s, :, :], k.R[:, tiles(g), :], ALU.add).then_inc(y_made, 1)
                    if t.live(3):
                        g, s = t.group(3), t.slot(3, 8)
                        dve.wait_ge(agg_in[s // 2], landed(t.turn(3, 8)))
                        V.tensor_tensor(agg[:, s, :, 0:C], agg[:, s, :, 0:C], a_rows, ALU.mult).then_inc(scaled, 1)

                steps(dve, step)

            @block.scalar
            def _(act):
                A = nc.scalar
                act.wait_ge(setup, 4)
                A.activation(sd[:, :], st[:, 1:2], ACT.Sqrt, bias=k.ln_eps[0:C, :]).then_inc(std_made, 1)
                act.wait_ge(setup, SETUP + 1)

                def step(t):
                    if t.live(3):
                        g, s = t.group(3), t.slot(3, 8)
                        act.wait_ge(agg_in[s // 2], landed(t.turn(3, 8)))
                        act.wait_ge(y_out[s // 2], landed(t.turn(3, 8)))
                        for j in range(G):
                            last = A.activation(y[:, s, j, :], c_row[:, :], ACT.Copy, scale=agg[:, s, j, C:C1])
                        last.then_inc(shifts_made, 1)

                steps(act, step)

            @block.tensor
            def _(pe):
                T = nc.tensor
                pe.wait_ge(setup, SETUP)
                T.matmul(ps_a[:, :], a_col[:, :], k.ident[0:C, 0:C], start=True, stop=True)
                T.matmul(ps_c[:, :], c_col[:, :], k.ident[0:C, 0:C], start=True, stop=True).then_inc(rows_made, 1)


def gnn_kernel(nc, d):
    with Phase(nc, "all") as ph:
        k = Kept()
        k.pool_mark, k.dve_mark = ph.sem("pool_mark"), ph.sem("dve_mark")
        k.R = ph.sb("x", [P, NT, C])
        k.src_row = ph.sb("src_row", [P, ET], INT32)
        k.dst_row = ph.sb("dst_row", [P, ET], INT32)
        k.dst_f = ph.sb("dst_f", [P, ET])
        k.scatter_row = ph.sb("scatter_row", [P, ET], INT32)
        k.ident = ph.sb("ident", [P, P])
        k.ln_eps = ph.sb("ln_eps", [P, 1])
        k.one_eps = ph.sb("one_eps", [P, 1])
        k.w_ef = ph.sb("w_ef", [CE, C])
        k.b_ef = ph.sb("b_ef", [C, 1])
        k.w_node = ph.sb("w_node", [C, C])
        k.b_node = ph.sb("b_node", [C, 1])
        k.w_msg = ph.sb("w_msg", [C, 3, C])
        k.b_msg = ph.sb("b_msg", [C1, C])
        k.w_ef_msg = ph.sb("w_ef_msg", [C1, C])
        k.bn_gb = ph.sb("bn_gb", [C, 6])
        k.u_bn = ph.sb("u_bn", [C, NG, 6])
        k.gram = ph.sb("gram", [C, C1])
        with Phase(nc, "layer0") as ph:
            k.mean = ph.sb("mean", [P, NT])
            k.rstd = ph.sb("rstd", [P, NT])
            k.w_e0 = ph.sb("w_e0", [C1, C])
            k.w1 = ph.sb("w1", [C, C])
            k.b1 = ph.sb("b1", [C, 1])
            k.w2 = ph.sb("w2", [C1, C])
            k.ef_bn = ph.sb("ef_bn", [C, EG, 6])
            edge_phase_0(nc, d, k)
            node_phase(nc, d, k)
        edge_phase_1(nc, d, k)
        final_phase(nc, d, k)


def kernel(x, src, dst, edge_attr_4, edge_attr_96, L0_gnn_W_edge, L0_gnn_b_edge, L0_gnn_eps, L0_gnn_W1, L0_gnn_b1,
           L0_gnn_W2, L0_gnn_b2, L1_gnn_W_node, L1_gnn_b_node, L1_gnn_g_node, L1_gnn_beta_node, L1_gnn_W_edge,
           L1_gnn_b_edge, L1_gnn_g_edge, L1_gnn_beta_edge, L1_gnn_W_msg, L1_gnn_b_msg, L1_gnn_g_msg, L1_gnn_beta_msg):
    import numpy as np
    from concourse import bacc
    from concourse.bass_utils import run_bass_kernel_spmd

    def table(a):
        padded = np.zeros((TILES * P, a.shape[1]), a.dtype)
        padded[:a.shape[0]] = a
        return np.ascontiguousarray(padded.reshape(TILES, P, -1).transpose(1, 0, 2))

    def edges(a, fill):
        padded = np.full(ET * P, fill, np.int32)
        padded[:EDGES] = a
        return padded

    def transposed(a):
        padded = np.zeros((a.shape[1], ET * P), a.dtype)
        padded[:, :EDGES] = np.asarray(a).T
        return padded

    def column(a):
        return np.asarray(a).reshape(-1, 1)

    x, src, dst = np.asarray(x), np.asarray(src), np.asarray(dst)
    src_p, dst_p = edges(src, 0), edges(dst, DUMP * P)
    arrays = {
        "x": table(x),
        "src_col": src_p.reshape(ET, P).T, "dst_col": dst_p.reshape(ET, P).T, "dst_row": dst_p.reshape(1, -1),
        "eaT": transposed(edge_attr_96), "ea4T": transposed(edge_attr_4),
        "w_e0": np.concatenate([np.asarray(L0_gnn_W_edge).T, np.asarray(L0_gnn_b_edge)[None]]),
        "eps": np.asarray(L0_gnn_eps).reshape(1, 1),
        "w1": np.asarray(L0_gnn_W1).T, "b1": column(L0_gnn_b1),
        "w2": np.concatenate([np.asarray(L0_gnn_W2).T, np.asarray(L0_gnn_b2)[None]]),
        "w_node": np.asarray(L1_gnn_W_node), "b_node": column(L1_gnn_b_node),
        "w_ef": np.asarray(L1_gnn_W_edge), "b_ef": column(L1_gnn_b_edge),
        "w_msg": np.asarray(L1_gnn_W_msg).reshape(3, C, C), "b_msg": np.asarray(L1_gnn_b_msg).reshape(1, C),
        "bn_gb": np.concatenate([column(a) for a in (L1_gnn_g_node, L1_gnn_beta_node, L1_gnn_g_edge, L1_gnn_beta_edge,
                                                     L1_gnn_g_msg, L1_gnn_beta_msg)], axis=1),
    }
    arrays = {n: np.ascontiguousarray(a) for n, a in arrays.items()}

    nc = bacc.Bacc("TRN2", target_bir_lowering=False, num_devices=1, dynamic_dma_scratch_size=4096)
    d = {n: nc.dram_tensor(f"in_{n}", a.shape, mybir.dt.from_np(a.dtype), kind="ExternalInput").ap()
         for n, a in arrays.items()}
    d["agg0"] = nc.dram_tensor("agg0", (P, TILES, C), FP32, kind="Internal").ap()
    d["agg1"] = nc.dram_tensor("agg1", (P, TILES, C1), FP32, kind="Internal").ap()
    d["h1"] = nc.dram_tensor("h1", (P, TILES, C), FP32, kind="Internal").ap()
    d["uT"] = nc.dram_tensor("uT", (C, NT * P), FP32, kind="Internal").ap()
    d["out"] = nc.dram_tensor("out", (P, NT, C), FP32, kind="ExternalOutput").ap()
    gnn_kernel(nc, d)
    got = run_bass_kernel_spmd(nc, [{f"in_{n}": a for n, a in arrays.items()}], core_ids=[0]).results[0]["out"]
    return np.asarray(got).transpose(1, 0, 2).reshape(NT * P, C)[:NODES]
```
